# Optimizing a Trainium2 kernel written in Bass

```python
import numpy as np
import jax
import jax.numpy as jnp

def _softmax(x, axis=-1):
    return jax.nn.softmax(x, axis=axis)

def _gelu(x):
    return jax.nn.gelu(x, approximate=True)

def _silu(x):
    return jax.nn.silu(x)

def _sigmoid(x):
    return jax.nn.sigmoid(x)

def _layernorm(x, axis=-1, eps=1e-05):
    m = jnp.mean(x, axis=axis, keepdims=True)
    v = jnp.var(x, axis=axis, keepdims=True)
    return (x - m) / jnp.sqrt(v + eps)

def _scatter_add(tgt, idx, src, axis=0):
    return tgt.at[idx].add(src)

def _segment_sum(src, seg, n):
    return jax.ops.segment_sum(src, seg, n)
kernel_name = 'mk_flamingo_gated_d1_seqx_r4_97c036'

def setup_inputs(seed: int=0):
    np.random.seed(seed)
    _w = jnp.asarray

    def _rec_inputs():
        import jax
        import jax.numpy as jnp
        _rk = jax.random.key(seed)
        x = 7.22e-05 + 1 * jax.random.normal(jax.random.fold_in(_rk, 1), (2, 1024, 256), jnp.float32)
        _lenS = 1024 - jax.random.randint(jax.random.fold_in(_rk, 7), (2,), 0, max(1, 1024 // 4) + 1, jnp.int32)
        _lenS2 = 77 - jax.random.randint(jax.random.fold_in(_rk, 8), (2,), 0, max(1, 77 // 4) + 1, jnp.int32)
        _ctx_1024P = jax.random.normal(jax.random.fold_in(_rk, 11), (2, 16, 256), jnp.float32)
        _ctx_1024c = jax.random.dirichlet(jax.random.fold_in(_rk, 511), 0.3 * jnp.ones((16,), jnp.float32), (2, 77))
        _ctx_1024t = jnp.einsum('bsk,bkd->bsd', _ctx_1024c, _ctx_1024P)
        _ctx_1024t = _ctx_1024t * jax.lax.rsqrt(jnp.mean(jnp.square(_ctx_1024t)) + 1e-12) * 0.953939
        ctx_1024 = 4.13588e-05 + 0.999923 * (_ctx_1024t + 0.3 * jax.random.normal(jax.random.fold_in(_rk, 611), (2, 77, 256), jnp.float32))
        _validS = jnp.arange(1024)[None, :] < _lenS[:, None]
        _validS2 = jnp.arange(77)[None, :] < _lenS2[:, None]
        _causal = jnp.tril(jnp.ones((1024, 1024), dtype=bool))
        mask_BxS2_bk0 = jnp.logical_not(jnp.broadcast_to(_validS2[:, :], (2, 77)))
        _g = jax.random.normal(jax.random.fold_in(_rk, 9001), (2, 1), jnp.float32)
        _g = jnp.sign(_g) * jnp.maximum(jnp.abs(_g), 1.0) + (_g == 0) * 1.0
        g_xattn = _g[0]
        g_ffn = _g[1]
        return (x, ctx_1024, mask_BxS2_bk0, g_xattn, g_ffn)
    x, ctx_1024, mask_BxS2_bk0, g_xattn, g_ffn = _rec_inputs()

    def _L0_xattn_setup():
        import jax, jax.numpy as jnp
        import numpy as np
        B, LQ, LK = (4, 512, 512)
        DQ = DK = DV = DH = 256

        def _xavier(key, shape):
            fan_out, fan_in = shape
            bound = float(np.sqrt(6.0 / (fan_in + fan_out)))
            return jax.random.uniform(key, shape, jnp.float32, -bound, bound)
        key = jax.random.key(seed)
        ks = jax.random.split(key, 6)
        query = jax.random.normal(ks[0], (B, LQ, DQ), jnp.float32)
        k_in = jax.random.normal(ks[1], (B, LK, DK), jnp.float32)
        key_mask = jax.random.randint(ks[2], (B, LK), 0, 2).astype(bool)
        Wk = _xavier(ks[3], (2 * DH, DK))
        bk = jnp.zeros((2 * DH,), jnp.float32)
        Wq = _xavier(ks[4], (DH, DQ))
        bq = jnp.zeros((DH,), jnp.float32)
        Wfc = _xavier(ks[5], (DV, DH))
        bfc = jnp.zeros((DV,), jnp.float32)
        return {'query': query, 'key': k_in, 'key_mask': key_mask, 'Wq': Wq, 'bq': bq, 'Wk': Wk, 'bk': bk, 'Wfc': Wfc, 'bfc': bfc}
    _L0_xattn_all = _L0_xattn_setup()
    _L0_xattn_in = {k: v for k, v in _L0_xattn_all.items() if k in ('Wq', 'bq', 'Wk', 'bk', 'Wfc', 'bfc')}
    del _L0_xattn_all

    def _L0_ffn_setup():
        import jax, jax.numpy as jnp
        import numpy as np
        import math
        D_IN = 256
        FEATURES = (1024, 1024, 256)
        BATCH, SEQ = (8, 512)

        def _conn_dense(kernel_bool, x):
            w = jnp.where(kernel_bool, jnp.float32(1.0), jnp.float32(-1.0))
            return x @ w
        key = jax.random.key(seed)
        kx, kk0, kk1, kk2 = jax.random.split(key, 4)
        x = jax.random.normal(kx, (BATCH, SEQ, D_IN), dtype=jnp.float32)
        k0 = jax.random.randint(kk0, (2 * D_IN, FEATURES[0]), 0, 2).astype(jnp.bool_)
        k1 = jax.random.randint(kk1, (FEATURES[0], FEATURES[1]), 0, 2).astype(jnp.bool_)
        k2 = jax.random.randint(kk2, (FEATURES[1], FEATURES[2]), 0, 2).astype(jnp.bool_)
        s0 = jnp.asarray(1.0 / math.sqrt(2 * D_IN), dtype=jnp.float32)
        s1 = jnp.asarray(1.0 / math.sqrt(FEATURES[0]), dtype=jnp.float32)
        s2 = jnp.asarray(1.0 / math.sqrt(FEATURES[1]), dtype=jnp.float32)
        return {'x': x, 'k0': k0, 'k1': k1, 'k2': k2, 's0': s0, 's1': s1, 's2': s2}
    _L0_ffn_all = _L0_ffn_setup()
    _L0_ffn_in = {k: v for k, v in _L0_ffn_all.items() if k in ('k0', 'k1', 'k2', 's0', 's1', 's2')}
    del _L0_ffn_all
    return {'x': x, 'ctx_1024': ctx_1024, 'mask_BxS2_bk0': mask_BxS2_bk0, 'g_xattn': g_xattn, 'g_ffn': g_ffn, 'L0_xattn_Wq': _L0_xattn_in['Wq'], 'L0_xattn_bq': _L0_xattn_in['bq'], 'L0_xattn_Wk': _L0_xattn_in['Wk'], 'L0_xattn_bk': _L0_xattn_in['bk'], 'L0_xattn_Wfc': _L0_xattn_in['Wfc'], 'L0_xattn_bfc': _L0_xattn_in['bfc'], 'L0_ffn_k0': _L0_ffn_in['k0'], 'L0_ffn_k1': _L0_ffn_in['k1'], 'L0_ffn_k2': _L0_ffn_in['k2'], 'L0_ffn_s0': _L0_ffn_in['s0'], 'L0_ffn_s1': _L0_ffn_in['s1'], 'L0_ffn_s2': _L0_ffn_in['s2']}

def reference(x, ctx_1024, mask_BxS2_bk0, g_xattn, g_ffn, L0_xattn_Wq, L0_xattn_bq, L0_xattn_Wk, L0_xattn_bk, L0_xattn_Wfc, L0_xattn_bfc, L0_ffn_k0, L0_ffn_k1, L0_ffn_k2, L0_ffn_s0, L0_ffn_s1, L0_ffn_s2):
    import jax
    import jax.numpy as jnp

    def _L0_xattn_ref(query, key, key_mask, Wq, bq, Wk, bk, Wfc, bfc):
        import jax, jax.numpy as jnp
        import numpy as np
        B, LQ, LK = (4, 512, 512)
        DQ = DK = DV = DH = 256

        def _xavier(key, shape):
            fan_out, fan_in = shape
            bound = float(np.sqrt(6.0 / (fan_in + fan_out)))
            return jax.random.uniform(key, shape, jnp.float32, -bound, bound)
        bs, timesteps, _ = key.shape
        dim = DH
        q = query @ Wq.T + bq
        c = (key @ Wk.T + bk).reshape(bs, timesteps, 2, dim)
        k = c[:, :, 0]
        v = c[:, :, 1]
        scores = jnp.einsum('bqd,bkd->bqk', q, k)
        scores = jnp.where(key_mask[:, None, :], -jnp.inf, scores)
        attn = jax.nn.softmax(scores, axis=-1)
        out = jnp.einsum('bqk,bkd->bqd', attn, v)
        out = out @ Wfc.T + bfc
        return out

    def _L0_ffn_ref(x, k0, k1, k2, s0, s1, s2):
        import jax, jax.numpy as jnp
        import numpy as np
        import math
        D_IN = 256
        FEATURES = (1024, 1024, 256)
        BATCH, SEQ = (8, 512)

        def _conn_dense(kernel_bool, x):
            w = jnp.where(kernel_bool, jnp.float32(1.0), jnp.float32(-1.0))
            return x @ w
        h = jnp.concatenate([x, -x], axis=-1)
        h = s0 * _conn_dense(k0, h)
        h = jax.nn.relu(h) * 2
        h = s1 * _conn_dense(k1, h)
        h = jax.nn.relu(h) * 2
        h = s2 * _conn_dense(k2, h)
        return h
    x = x + jnp.tanh(g_xattn[0]) * _L0_xattn_ref(_layernorm(x, axis=-1), ctx_1024, mask_BxS2_bk0, L0_xattn_Wq, L0_xattn_bq, L0_xattn_Wk, L0_xattn_bk, L0_xattn_Wfc, L0_xattn_bfc)
    x = x + jnp.tanh(g_ffn[0]) * _L0_ffn_ref(_layernorm(x, axis=-1), L0_ffn_k0, L0_ffn_k1, L0_ffn_k2, L0_ffn_s0, L0_ffn_s1, L0_ffn_s2)
    return x

_drawn_inputs = setup_inputs


def setup_inputs(seed=0):
    import zlib

    import numpy as np

    out = dict(_drawn_inputs(seed))
    spreads = {'L0_xattn_bq': (0.0, 0.1), 'L0_xattn_bk': (0.0, 0.1), 'L0_xattn_bfc': (0.0, 0.1)}
    factors = {}
    for name, (base, spread) in spreads.items():
        noise = np.random.default_rng([zlib.crc32(name.encode()), seed]).standard_normal(out[name].shape)
        drawn = base * np.exp(spread * noise) if base else spread * noise
        out[name] = jnp.asarray(drawn.astype(out[name].dtype))
    for name, factor in factors.items():
        out[name] = (out[name] * factor).astype(out[name].dtype)
    return out
```

```python
from contextlib import ExitStack

import numpy as np

import concourse.bass as bass
from concourse import mybir

P = 128
B, S, D, L, H = 2, 1024, 256, 77, 1024
CHUNK = 512
NC = B * S // CHUNK
CB = S // CHUNK
T = CHUNK // P
KD = D // P
KH = H // P
BL = B * L
HB = 2 * KH
TB = 512 // D
NF = 4

N_SCALE = 2.0 ** 10
W0_SCALE = 2.0 ** -4
W1_SCALE = 2.0 ** -10
OUT_SCALE = 4.0 / (N_SCALE * W0_SCALE * W1_SCALE)
MASKED = -1e30
EPS = 1e-5
RSQRT_GUESS = float(0x5F3759DF)
LN_STEPS = 3 + 3 * 3
ATTEND_STEPS = 2 * LN_STEPS + 8


def flamingo_kernel(nc, x, xT, ctxT, wkT, wq, wfcT, bias_cols, bfc, mask, scalars, k0, k1, k2, out):
    f32, f16, u8, i32 = mybir.dt.float32, mybir.dt.float16, mybir.dt.uint8, mybir.dt.int32
    ALU, ACT, AX = mybir.AluOpType, mybir.ActivationFunctionType, mybir.AxisListType

    x_rows = x.rearrange("(c p t) d -> p c t d", c=NC, p=P)
    out_rows = out.rearrange("(c p t) d -> p c t d", c=NC, p=P)

    ctx = ExitStack()
    with ctx:
        def sb(name, shape, dt=f32):
            return ctx.enter_context(nc.sbuf_tensor(name, shape, dt))

        def sem(name):
            return ctx.enter_context(nc.semaphore(name))

        x_sb = sb("x_sb", [P, NC, T, D])
        xT_sb = sb("xT_sb", [P, KD, CHUNK])
        ctxT_sb = sb("ctxT_sb", [P, KD, BL])
        wkT_sb = sb("wkT_sb", [P, KD, 2 * D])
        wq_sb = sb("wq_sb", [P, KD, D])
        wfcT_sb = sb("wfcT_sb", [P, KD, D])
        cols = sb("cols", [P, 6])
        bfc_sb = sb("bfc_sb", [L, D])
        mask_sb = sb("mask_sb", [P, BL], u8)
        scal = sb("scal", [P, 5])
        k0_sb = sb("k0_sb", [P, 2 * KD, H], u8)
        k1_sb = sb("k1_sb", [P, KH, H], u8)
        k2_sb = sb("k2_sb", [P, KH, D], u8)

        W0 = sb("W0", [P, KD, H], f16)
        W0_bottom = sb("W0_bottom", [P, KD, H], f16)
        W1 = sb("W1", [P, KH, H], f16)
        W2 = sb("W2", [P, KH, D], f16)

        ident = sb("ident", [P, P])
        ones = sb("ones", [P, P])
        wq_mean = sb("wq_mean", [P, 2, KD])
        wqc = sb("wqc", [P, KD, D])
        bq_wide = sb("bq_wide", [P, KD, P])
        KT = sb("KT", [P, KD, BL])
        VT = sb("VT", [P, KD, BL])
        G = sb("G", [P, KD, NC, L])
        key_bias = sb("key_bias", [P, NC, L])
        V2 = sb("V2", [L, NC, D])
        gates = sb("gates", [P, 2])
        gate_x = sb("gate_x", [P, NC])
        all_masked = sb("all_masked", [P, 4, B])
        signs = sb("signs", [P, 3, 2])
        weight_scale = sb("weight_scale", [P, 5])
        out_gate = sb("out_gate", [P, 3])

        stats = sb("stats", [P, T, 6])
        mean_var = sb("mean_var", [P, T, 2])
        rs_var = sb("rs_var", [P, T])
        rs_half = sb("rs_half", [P, T], i32)
        rs_y = sb("rs_y", [P, 4, T])
        rs_t = sb("rs_t", [P, 2, T])
        wait_bearer = sb("wait_bearer", [P, 1])
        rstd_q = sb("rstd_q", [P, T])
        scores = sb("scores", [P, T, L])
        neg_max = sb("neg_max", [P, T])
        probs = sb("probs", [P, T, L])
        prob_sum = sb("prob_sum", [P, T])
        row_scale = sb("row_scale", [P, 2, T])
        probsT = sb("probsT", [L, CHUNK])
        xn = sb("xn", [P, T, D])

        nT = [sb(f"nT_{h}", [P, KD, CHUNK], f16) for h in ("hi", "lo")]
        h1 = [sb(f"h1_{h}", [P, KH, CHUNK], f16) for h in ("hi", "lo")]
        h2 = [sb(f"h2_{h}", [P, KH, CHUNK], f16) for h in ("hi", "lo")]

        hid = [ctx.enter_context(nc.psum_tensor(f"hid{i}", [P, 512], f32)) for i in range(NF)]
        aux = [ctx.enter_context(nc.psum_tensor(f"aux{i}", [P, 512], f32)) for i in range(4)]
        ps_K, ps_V, ps_G, ps_qb = (h[:, 0:BL * n].rearrange("p (a b) -> p a b", a=n)
                                   for h, n in zip(hid, (KD, KD, KD, 1)))
        ps_V2 = aux[2]
        ps_scores = aux[0][:, 0:T * L].rearrange("p (t l) -> p t l", t=T)
        ps_probsT = aux[1]
        ps_nT = aux[0:2]
        ps_rows = [aux[2 + t // TB][:, (t % TB) * D:(t % TB + 1) * D] for t in range(T)]

        ctx_in, wk_in, wv_in, wq_in, wfc_in = sem("ctx_in"), sem("wk_in"), sem("wv_in"), sem("wq_in"), sem("wfc_in")
        cols_in, scal_in, mask_in, bfc_in = sem("cols_in"), sem("scal_in"), sem("mask_in"), sem("bfc_in")
        x_in = [sem(f"x_in{c}") for c in range(NC)]
        xT_in = sem("xT_in")
        k0_in, k1_in, k2_in = sem("k0_in"), [sem(f"k1_in{i}") for i in range(2)], sem("k2_in")
        ident_step = sem("ident_step")
        ones_set = sem("ones_set")
        setup_step = sem("setup_step")
        wqc_done, bq_wide_done = sem("wqc_done"), sem("bq_wide_done")
        kv_mm = sem("kv_mm")
        KT_done, VT_done, G_done, V2_done = sem("KT_done"), sem("VT_done"), sem("G_done"), sem("V2_done")
        gates_done, weight_scale_done = sem("gates_done"), sem("weight_scale_done")
        W0_bottom_done, W0_done, W1_done, W2_done = (sem("W0_bottom_done"), sem("W0_done"),
                                                     sem("W1_done"), sem("W2_done"))
        attend_step = sem("attend_step")
        scores_mm, neg_max_done, probs_done = sem("scores_mm"), sem("neg_max_done"), sem("probs_done")
        probsT_mm, probsT_done, values_mm = sem("probsT_mm"), sem("probsT_done"), sem("values_mm")
        xn_done, nT_mm, nT_hi_done, nT_lo_done = (sem("xn_done"), sem("nT_mm"), sem("nT_hi_done"),
                                                  sem("nT_lo_done"))
        hidden_mm, hi_done, lo_done = sem("hidden_mm"), sem("hi_done"), sem("lo_done")
        rows_mm, rows_done = sem("rows_mm"), sem("rows_done")
        stored = sem("stored")

        block = ctx.enter_context(nc.Block())

        @block.sync
        def _(sp):
            sp.dma_start(ctxT_sb[:], ctxT).then_inc(ctx_in, 16)
            sp.dma_start(wkT_sb[:, :, 0:D], wkT[:, :, 0:D]).then_inc(wk_in, 16)
            sp.dma_start(xT_sb[:], xT[:, 0]).then_inc(xT_in, 16)
            sp.dma_start(x_sb[:, 0], x_rows[:, 0]).then_inc(x_in[0], 16)
            sp.dma_start(wkT_sb[:, :, D:2 * D], wkT[:, :, D:2 * D]).then_inc(wv_in, 16)
            sp.dma_start(wfcT_sb[:], wfcT).then_inc(wfc_in, 16)
            for i in range(2):
                half = slice(i * KH // 2, (i + 1) * KH // 2)
                sp.dma_start(k1_sb[:, half], k1[:, half]).then_inc(k1_in[i], 16)
            sp.dma_start(k2_sb[:], k2).then_inc(k2_in, 16)
            for c in range(1, NC):
                sp.dma_start(x_sb[:, c], x_rows[:, c]).then_inc(x_in[c], 16)
            with sp.Fori(0, NC - 1) as c:
                sp.wait_ge(scores_mm, c + 1)
                sp.dma_start(xT_sb[:], xT[:, bass.ds(c + 1, 1)]).then_inc(xT_in, 16)
                sp.wait_ge(rows_done, T * c + T)
                sp.dma_start(out_rows[:, bass.ds(c, 1)], x_sb[:, bass.ds(c, 1)]).then_inc(stored, 16)
            for t in range(T):
                sp.wait_ge(rows_done, T * (NC - 1) + t + 1)
                sp.dma_start(out_rows[:, NC - 1, t], x_sb[:, NC - 1, t]).then_inc(stored, 16)
            sp.wait_ge(stored, 16 * (NC - 1 + T))

        @block.gpsimd
        def _(pool):
            nc.gpsimd.memset(ones[:], 1.0).then_inc(ones_set, 1)
            nc.gpsimd.memset(ident[:], 0.0).then_inc(ident_step, 1)
            pool.wait_ge(ident_step, 1)
            nc.gpsimd.affine_select(out=ident[:], in_=ident[:], compare_op=ALU.not_equal, fill=1.0, base=0,
                                    pattern=[[-1, P]], channel_multiplier=1).then_inc(ident_step, 1)
            pool.wait_ge(weight_scale_done, 1)
            for k in range(KH):
                if k % (KH // 2) == 0:
                    pool.wait_ge(k1_in[k // (KH // 2)], 16)
                nc.gpsimd.tensor_scalar(W1[:, k], k1_sb[:, k], weight_scale[:, 2:3], weight_scale[:, 3:4],
                                        ALU.mult, ALU.add).then_inc(W1_done, 1)
            pool.wait_ge(k2_in, 16)
            nc.gpsimd.tensor_scalar(W2[:], k2_sb[:], 2.0, -1.0, ALU.mult, ALU.add).then_inc(W2_done, 1)

        @block.scalar
        def _(act):
            act.dma_start(wq_sb[:], wq).then_inc(wq_in, 16)
            act.dma_start(cols[:], bias_cols).then_inc(cols_in, 16)
            act.dma_start(scal[:], scalars.partition_broadcast(P)).then_inc(scal_in, 16)
            act.dma_start(mask_sb[:], mask.partition_broadcast(P)).then_inc(mask_in, 16)
            act.dma_start(bfc_sb[:], bfc.partition_broadcast(L)).then_inc(bfc_in, 16)
            act.dma_start(k0_sb[:], k0).then_inc(k0_in, 16)
            act.preload_act_table(ACT.Exp)

            def exponentials(c):
                act.wait_ge(neg_max_done, c + 1)
                for t in range(T):
                    nc.scalar.activation(probs[:, t], scores[:, t], ACT.Exp, bias=neg_max[:, t:t + 1], scale=1.0,
                                         accum_out=prob_sum[:, t:t + 1]).then_inc(probs_done, 1)

            def copy_probsT(c):
                act.wait_ge(probsT_mm, c + 1)
                nc.scalar.activation(probsT[:], ps_probsT[0:L, :], ACT.Copy).then_inc(probsT_done, 1)

            def split_hi(c):
                for k in range(KD):
                    act.wait_ge(nT_mm, KD * c + k + 1)
                    nc.scalar.activation(nT[0][:, k], ps_nT[k][:, :], ACT.Copy, scale=N_SCALE).then_inc(nT_hi_done, 1)

            def mlp(c, attend_next):
                for n in range(HB):
                    h = (h1, h2)[n // KH][0]
                    act.wait_ge(hidden_mm, HB * c + n + 1)
                    nc.scalar.activation(h[:, n % KH], hid[n % NF][:, :], ACT.Relu).then_inc(hi_done, 1)
                    if attend_next and n == 10:
                        exponentials(c + 1)
                    if attend_next and n == 11:
                        copy_probsT(c + 1)
                    if attend_next and n == 14:
                        split_hi(c + 1)

            act.wait_ge(cols_in, 16)
            act.wait_ge(kv_mm, 1)
            for m in range(KD):
                nc.scalar.activation(KT[:, m], ps_K[:, m], ACT.Identity, bias=cols[:, m:m + 1]).then_inc(KT_done, 1)
            act.wait_ge(scal_in, 16)
            nc.scalar.activation(gates[:], scal[:, 0:2], ACT.Tanh).then_inc(gates_done, 1)
            act.wait_ge(kv_mm, 2)
            for b in range(B):
                for i in range(CB):
                    nc.scalar.activation(G[:, :, b * CB + i], ps_G[:, :, b * L:(b + 1) * L],
                                         ACT.Copy).then_inc(G_done, 1)
            act.wait_ge(kv_mm, 4)
            for m in range(KD):
                nc.scalar.activation(VT[:, m], ps_V[:, m], ACT.Identity,
                                     bias=cols[:, KD + m:KD + m + 1]).then_inc(VT_done, 1)
            act.wait_ge(k0_in, 16)
            act.wait_ge(weight_scale_done, 1)
            nc.scalar.activation(W0_bottom[:], k0_sb[:, KD:2 * KD], ACT.Copy,
                                 scale=weight_scale[:, 1:2]).then_inc(W0_bottom_done, 1)
            exponentials(0)
            copy_probsT(0)
            split_hi(0)
            with act.Fori(0, NC - 1) as c:
                mlp(c, True)
            mlp(NC - 1, False)

        @block.vector
        def _(dve):
            V = nc.vector

            def rsqrt_rows(base, dst):
                V.tensor_scalar(rs_var[:], mean_var[:, :, 1], EPS, None, ALU.add).then_inc(attend_step, 1)
                dve.wait_ge(attend_step, base + 1)
                V.tensor_scalar(rs_half[:], rs_var[:].bitcast(i32), 1, None,
                                ALU.logical_shift_right).then_inc(attend_step, 1)
                dve.wait_ge(attend_step, base + 2)
                V.tensor_scalar(rs_y[:, 0].bitcast(i32), rs_half[:], -1.0, RSQRT_GUESS,
                                ALU.mult, ALU.add).then_inc(attend_step, 1)
                for i in range(3):
                    y = rs_y[:, i]
                    dve.wait_ge(attend_step, base + 3 * i + 3)
                    V.tensor_tensor(rs_t[:, 0], y, y, ALU.mult).then_inc(attend_step, 1)
                    dve.wait_ge(attend_step, base + 3 * i + 4)
                    V.scalar_tensor_tensor(rs_t[:, 1], rs_t[:, 0], -0.5, rs_var[:],
                                           ALU.mult, ALU.mult).then_inc(attend_step, 1)
                    dve.wait_ge(attend_step, base + 3 * i + 5)
                    V.scalar_tensor_tensor(dst if i == 2 else rs_y[:, i + 1], rs_t[:, 1], 1.5, y,
                                           ALU.add, ALU.mult).then_inc(attend_step, 1)

            def rows_of(c, t):
                return x_sb[:, c, t] if isinstance(c, int) else x_sb[:, bass.ds(c, 1), t]

            def query_rstd(c):
                base = ATTEND_STEPS * c
                for t in range(T):
                    last = V.bn_stats(stats[:, t], rows_of(c, t))
                last.then_inc(attend_step, 1)
                dve.wait_ge(attend_step, base + 1)
                V.tensor_copy(wait_bearer[:], scal[:, 0:1])
                for t in range(T):
                    last = V.bn_aggr(mean_var[:, t], stats[:, t])
                last.then_inc(attend_step, 1)
                dve.wait_ge(attend_step, base + 2)
                rsqrt_rows(base + 2, rstd_q[:])

            def softmax_max(c):
                base = ATTEND_STEPS * c + 2 + LN_STEPS
                dve.wait_ge(attend_step, base)
                dve.wait_ge(scores_mm, c + 1)
                bias = key_bias[:, c] if isinstance(c, int) else key_bias[:, bass.ds(c, 1)]
                for t in range(T):
                    last = V.scalar_tensor_tensor(scores[:, t], ps_scores[:, t], rstd_q[:, t:t + 1], bias,
                                                  ALU.mult, ALU.add)
                last.then_inc(attend_step, 1)
                dve.wait_ge(attend_step, base + 1)
                V.reduce_max(neg_max[:], scores[:], AX.X, negate=True).then_inc(neg_max_done, 1)

            def residual_and_norm(c):
                base = ATTEND_STEPS * c + 3 + LN_STEPS
                dve.wait_ge(probs_done, T * c + T)
                V.reciprocal(row_scale[:, 0], prob_sum[:]).then_inc(attend_step, 1)
                dve.wait_ge(attend_step, base + 1)
                gate = gate_x[:, c:c + 1] if isinstance(c, int) else gate_x[:, bass.ds(c, 1)]
                V.tensor_scalar(row_scale[:, 1], row_scale[:, 0], gate, None, ALU.mult).then_inc(attend_step, 1)
                dve.wait_ge(attend_step, base + 2)
                for t in range(T):
                    if t % TB == 0:
                        dve.wait_ge(values_mm, T // TB * c + t // TB + 1)
                    last = V.scalar_tensor_tensor(rows_of(c, t), ps_rows[t], row_scale[:, 1, t:t + 1], rows_of(c, t),
                                                  ALU.mult, ALU.add)
                last.then_inc(attend_step, 1)
                dve.wait_ge(attend_step, base + 3)
                V.tensor_copy(wait_bearer[:], scal[:, 0:1])
                for t in range(T):
                    last = V.bn_stats(stats[:, t], rows_of(c, t))
                last.then_inc(attend_step, 1)
                dve.wait_ge(attend_step, base + 4)
                V.tensor_copy(wait_bearer[:], scal[:, 0:1])
                for t in range(T):
                    last = V.bn_aggr(mean_var[:, t], stats[:, t])
                last.then_inc(attend_step, 1)
                dve.wait_ge(attend_step, base + 5)
                rsqrt_rows(base + 5, row_scale[:, 0])
                dve.wait_ge(attend_step, base + 5 + LN_STEPS)
                for t in range(T):
                    V.tensor_scalar(xn[:, t], rows_of(c, t), mean_var[:, t, 0:1], row_scale[:, 0, t:t + 1],
                                    ALU.subtract, ALU.mult).then_inc(xn_done, 1)

            def split_lo(c):
                for k in range(KD):
                    dve.wait_ge(nT_hi_done, KD * c + k + 1)
                    V.scalar_tensor_tensor(nT[1][:, k], ps_nT[k][:, :], N_SCALE, nT[0][:, k],
                                           ALU.mult, ALU.subtract).then_inc(nT_lo_done, 1)

            def mlp(c, attend_next):
                for n in range(HB):
                    hi, lo = (h1, h2)[n // KH]
                    dve.wait_ge(hi_done, HB * c + n + 1)
                    V.scalar_tensor_tensor(lo[:, n % KH], hid[n % NF][:, :], 0.0, hi[:, n % KH],
                                           ALU.max, ALU.subtract).then_inc(lo_done, 1)
                    if attend_next and n == 8:
                        query_rstd(c + 1)
                    if attend_next and n == 9:
                        softmax_max(c + 1)
                    if attend_next and n == 12:
                        residual_and_norm(c + 1)
                    if attend_next and n == 14:
                        split_lo(c + 1)
                for t in range(T):
                    if t % TB == 0:
                        dve.wait_ge(rows_mm, T // TB * c + t // TB + 1)
                    V.scalar_tensor_tensor(rows_of(c, t), ps_rows[t], out_gate[:, 2:3], rows_of(c, t),
                                           ALU.mult, ALU.add).then_inc(rows_done, 1)

            dve.wait_ge(scal_in, 16)
            V.tensor_scalar(signs[:, 0], scal[:, 2:4], 0.0, None, ALU.is_lt).then_inc(setup_step, 1)
            dve.wait_ge(setup_step, 1)
            V.scalar_tensor_tensor(signs[:, 1], scal[:, 2:4], 0.0, signs[:, 0],
                                   ALU.is_gt, ALU.subtract).then_inc(setup_step, 1)
            dve.wait_ge(setup_step, 2)
            V.tensor_scalar(weight_scale[:, 0:1], signs[:, 1, 0:1], 2 * W0_SCALE, None, ALU.mult)
            V.tensor_scalar(weight_scale[:, 1:2], signs[:, 1, 0:1], -2 * W0_SCALE, None, ALU.mult)
            V.tensor_scalar(weight_scale[:, 2:3], signs[:, 1, 1:2], 2 * W1_SCALE, None, ALU.mult)
            V.tensor_scalar(weight_scale[:, 3:4], signs[:, 1, 1:2], -W1_SCALE, None,
                            ALU.mult).then_inc(weight_scale_done, 1)
            V.tensor_tensor(signs[:, 2], signs[:, 1], scal[:, 2:4], ALU.mult).then_inc(setup_step, 1)
            dve.wait_ge(setup_step, 3)
            V.scalar_tensor_tensor(out_gate[:, 0:1], signs[:, 2, 0:1], OUT_SCALE, signs[:, 2, 1:2],
                                   ALU.mult, ALU.mult).then_inc(setup_step, 1)
            dve.wait_ge(setup_step, 4)
            V.tensor_tensor(out_gate[:, 1:2], out_gate[:, 0:1], scal[:, 4:5], ALU.mult).then_inc(setup_step, 1)

            dve.wait_ge(wq_in, 16)
            V.reduce_sum(wq_mean[:, 0], wq_sb[:], AX.X).then_inc(setup_step, 1)
            dve.wait_ge(setup_step, 6)
            V.tensor_scalar(wq_mean[:, 1], wq_mean[:, 0], -1.0 / D, None, ALU.mult).then_inc(setup_step, 1)
            dve.wait_ge(setup_step, 7)
            for k in range(KD):
                V.tensor_scalar(wqc[:, k], wq_sb[:, k], wq_mean[:, 1, k:k + 1], None,
                                ALU.add).then_inc(wqc_done, 1)
            dve.wait_ge(cols_in, 16)
            dve.wait_ge(ones_set, 1)
            for k in range(KD):
                V.tensor_scalar(bq_wide[:, k], ones[:], cols[:, 2 * KD + k:2 * KD + k + 1], None,
                                ALU.mult).then_inc(bq_wide_done, 1)
            dve.wait_ge(mask_in, 16)
            V.tensor_reduce(all_masked[:, 0], mask_sb[:].rearrange("p (b l) -> p b l", b=B), AX.X,
                            ALU.min).then_inc(setup_step, 1)
            dve.wait_ge(setup_step, 8)
            V.tensor_scalar(all_masked[:, 1], all_masked[:, 0], -1.0, 1.0, ALU.mult, ALU.add).then_inc(setup_step, 1)
            dve.wait_ge(setup_step, 9)
            V.reciprocal(all_masked[:, 2], all_masked[:, 1]).then_inc(setup_step, 1)
            dve.wait_ge(setup_step, 10)
            V.tensor_tensor(all_masked[:, 3], all_masked[:, 2], all_masked[:, 2], ALU.subtract).then_inc(setup_step, 1)
            dve.wait_ge(setup_step, 11)
            dve.wait_ge(gates_done, 1)
            for c in range(NC):
                V.tensor_tensor(gate_x[:, c:c + 1], all_masked[:, 3, c // CB:c // CB + 1], gates[:, 0:1], ALU.add)
            V.tensor_tensor(out_gate[:, 2:3], out_gate[:, 1:2], gates[:, 1:2], ALU.mult).then_inc(setup_step, 1)

            dve.wait_ge(x_in[0], 16)
            query_rstd(0)
            dve.wait_ge(kv_mm, 3)
            for c in range(NC):
                keys = slice(c // CB * L, (c // CB + 1) * L)
                last = V.scalar_tensor_tensor(key_bias[:, c], mask_sb[:, keys], MASKED, ps_qb[:, 0, keys],
                                              ALU.mult, ALU.add)
            last.then_inc(setup_step, 1)
            dve.wait_ge(setup_step, 13)
            softmax_max(0)
            dve.wait_ge(bfc_in, 16)
            dve.wait_ge(kv_mm, 5)
            for c in range(NC):
                V.tensor_tensor(V2[:, c], ps_V2[0:L, c // CB * D:(c // CB + 1) * D], bfc_sb[:],
                                ALU.add).then_inc(V2_done, 1)
            dve.wait_ge(W0_bottom_done, 1)
            V.scalar_tensor_tensor(W0[:], k0_sb[:, 0:KD], weight_scale[:, 0:1], W0_bottom[:],
                                   ALU.mult, ALU.add).then_inc(W0_done, 1)
            residual_and_norm(0)
            split_lo(0)
            for c in range(1, NC):
                dve.wait_ge(x_in[c], 16)
            with dve.Fori(0, NC - 1) as c:
                mlp(c, True)
            mlp(NC - 1, False)

        @block.tensor
        def _(pe):
            def query_scores(c):
                pe.wait_ge(xT_in, 16 * c + 16)
                for t in range(T):
                    for k in range(KD):
                        g = G[:, k, c] if isinstance(c, int) else G[:, k, bass.ds(c, 1)]
                        last = nc.tensor.matmul(ps_scores[:, t], xT_sb[:, k, t * P:(t + 1) * P], g,
                                                start=(k == 0), stop=(k == KD - 1))
                last.then_inc(scores_mm, 1)

            def transpose_probs(c):
                for t in range(T):
                    pe.wait_ge(probs_done, T * c + t + 1)
                    last = nc.tensor.transpose(ps_probsT[0:L, t * P:(t + 1) * P], probs[:, t], ident[:])
                last.then_inc(probsT_mm, 1)

            def attend_values(c):
                pe.wait_ge(probsT_done, c + 1)
                v2 = V2[:, c] if isinstance(c, int) else V2[:, bass.ds(c, 1)]
                for t in range(T):
                    last = nc.tensor.matmul(ps_rows[t][:, :], probsT[:, t * P:(t + 1) * P], v2,
                                            start=True, stop=True)
                    if t % TB == TB - 1:
                        last.then_inc(values_mm, 1)

            def transpose_xn(c):
                pe.wait_ge(xn_done, T * c + T)
                for k in range(KD):
                    for t in range(T):
                        last = nc.tensor.transpose(ps_nT[k][:, t * P:(t + 1) * P], xn[:, t, k * P:(k + 1) * P],
                                                   ident[:])
                    last.then_inc(nT_mm, 1)

            def mlp(c, attend_next):
                pe.wait_ge(nT_lo_done, KD * c + KD)
                for m in range(KH):
                    if m >= NF:
                        pe.wait_ge(lo_done, HB * c + m - NF + 1)
                    for k in range(KD):
                        for half in range(2):
                            last = nc.tensor.matmul(hid[m % NF][:, :], W0[:, k, m * P:(m + 1) * P], nT[half][:, k],
                                                    start=(k == 0 and half == 0), stop=(k == KD - 1 and half == 1))
                    last.then_inc(hidden_mm, 1)
                for m in range(KH):
                    if attend_next and m == 1:
                        query_scores(c + 1)
                    if attend_next and m == 4:
                        transpose_probs(c + 1)
                    if attend_next and m == 5:
                        attend_values(c + 1)
                    if attend_next and m == 7:
                        transpose_xn(c + 1)
                    if m > 0:
                        pe.wait_ge(lo_done, HB * c + KH + m - NF + 1)
                    for k in range(KH):
                        if m == 0:
                            pe.wait_ge(lo_done, HB * c + max(k + 1, KH - NF + 1))
                        if isinstance(c, int) and c == 0 and m == 0:
                            pe.wait_ge(W1_done, k + 1)
                        for half in range(2):
                            last = nc.tensor.matmul(hid[m % NF][:, :], W1[:, k, m * P:(m + 1) * P], h1[half][:, k],
                                                    start=(k == 0 and half == 0), stop=(k == KH - 1 and half == 1))
                    last.then_inc(hidden_mm, 1)
                for t in range(T):
                    for k in range(KH):
                        if t == 0:
                            pe.wait_ge(lo_done, HB * c + KH + k + 1)
                        for half in range(2):
                            last = nc.tensor.matmul(ps_rows[t][:, :], h2[half][:, k, t * P:(t + 1) * P], W2[:, k],
                                                    start=(k == 0 and half == 0), stop=(k == KH - 1 and half == 1))
                    if t % TB == TB - 1:
                        last.then_inc(rows_mm, 1)

            pe.wait_ge(ctx_in, 16)
            pe.wait_ge(wk_in, 16)
            for m in range(KD):
                for k in range(KD):
                    last = nc.tensor.matmul(ps_K[:, m], wkT_sb[:, k, m * P:(m + 1) * P], ctxT_sb[:, k],
                                            start=(k == 0), stop=(k == KD - 1))
            last.then_inc(kv_mm, 1)
            pe.wait_ge(wqc_done, KD)
            pe.wait_ge(KT_done, KD)
            for m in range(KD):
                for k in range(KD):
                    last = nc.tensor.matmul(ps_G[:, m], wqc[:, k, m * P:(m + 1) * P], KT[:, k],
                                            start=(k == 0), stop=(k == KD - 1))
            last.then_inc(kv_mm, 1)
            pe.wait_ge(bq_wide_done, KD)
            for k in range(KD):
                last = nc.tensor.matmul(ps_qb[:, 0], bq_wide[:, k], KT[:, k], start=(k == 0), stop=(k == KD - 1))
            last.then_inc(kv_mm, 1)
            pe.wait_ge(wv_in, 16)
            for m in range(KD):
                for k in range(KD):
                    last = nc.tensor.matmul(ps_V[:, m], wkT_sb[:, k, D + m * P:D + (m + 1) * P], ctxT_sb[:, k],
                                            start=(k == 0), stop=(k == KD - 1))
            last.then_inc(kv_mm, 1)
            pe.wait_ge(G_done, NC)
            query_scores(0)
            pe.wait_ge(wfc_in, 16)
            pe.wait_ge(VT_done, KD)
            for b in range(B):
                for k in range(KD):
                    last = nc.tensor.matmul(ps_V2[0:L, b * D:(b + 1) * D], VT[:, k, b * L:(b + 1) * L], wfcT_sb[:, k],
                                            start=(k == 0), stop=(k == KD - 1))
            last.then_inc(kv_mm, 1)
            pe.wait_ge(ident_step, 2)
            transpose_probs(0)
            pe.wait_ge(V2_done, NC)
            attend_values(0)
            transpose_xn(0)
            pe.wait_ge(W0_done, 1)
            pe.wait_ge(W1_done, KH)
            pe.wait_ge(W2_done, 1)
            with pe.Fori(0, NC - 1) as c:
                mlp(c, True)
            mlp(NC - 1, False)


def kernel(**inputs):
    import concourse.bacc as bacc
    from concourse.bass_utils import run_bass_kernel_spmd

    a = {name: np.asarray(v) for name, v in inputs.items()}

    def tiles(m):
        return np.ascontiguousarray(m.reshape(m.shape[0] // P, P, m.shape[1]).transpose(1, 0, 2))

    x = a["x"].reshape(B * S, D)
    arrays = {
        "x": x,
        "xT": x.reshape(NC, P, T, KD, P).transpose(4, 0, 3, 2, 1).reshape(P, NC, KD, CHUNK),
        "ctxT": tiles(a["ctx_1024"].reshape(BL, D).T),
        "wkT": tiles(a["L0_xattn_Wk"].T),
        "wq": tiles(a["L0_xattn_Wq"]),
        "wfcT": tiles(a["L0_xattn_Wfc"].T),
        "bias_cols": np.concatenate([a["L0_xattn_bk"].reshape(-1, P).T, a["L0_xattn_bq"].reshape(-1, P).T], 1),
        "bfc": a["L0_xattn_bfc"],
        "mask": a["mask_BxS2_bk0"].reshape(BL),
        "scalars": np.concatenate([a[n].reshape(1) for n in
                                   ("g_xattn", "g_ffn", "L0_ffn_s0", "L0_ffn_s1", "L0_ffn_s2")]),
        "k0": tiles(a["L0_ffn_k0"]),
        "k1": tiles(a["L0_ffn_k1"]),
        "k2": tiles(a["L0_ffn_k2"]),
    }
    arrays = {n: np.ascontiguousarray(v) for n, v in arrays.items()}
    nc = bacc.Bacc("TRN2", target_bir_lowering=False, num_devices=1)
    args = [nc.dram_tensor(n, v.shape, mybir.dt.from_np(v.dtype), kind="ExternalInput").ap()
            for n, v in arrays.items()]
    out = nc.dram_tensor("out", (B * S, D), mybir.dt.float32, kind="ExternalOutput").ap()
    flamingo_kernel(nc, *args, out)
    r = run_bass_kernel_spmd(nc, [arrays], core_ids=[0])
    return r.results[0]["out"].reshape(B, S, D)
```

```python
from contextlib import ExitStack

import numpy as np

import concourse.bass as bass
from concourse import mybir

P = 128
B, S, D, L, H = 2, 1024, 256, 77, 1024
CHUNK = 512
NC = B * S // CHUNK
CB = S // CHUNK
T = CHUNK // P
KD = D // P
KH = H // P
BL = B * L
HB = 2 * KH
TB = 512 // D
HALVES = T // TB
HALF = CHUNK // HALVES
W1_BY_ACT = 3
WARM_UP = 9
NF = 4

N_SCALE = 2.0 ** 10
W0_SCALE = 2.0 ** -4
W1_SCALE = 2.0 ** -10
OUT_SCALE = 4.0 / (N_SCALE * W0_SCALE * W1_SCALE)
MASKED = -1e30
EPS = 1e-5
RSTD_STEPS = 5
X1_STEP = 2 + RSTD_STEPS + HALVES + 3
ATTEND_STEPS = 2 * (2 + RSTD_STEPS) + HALVES + 3


def flamingo_kernel(nc, x, xT, ctxT, wkT, wvT, wq, wfcT, bias_cols, bfc, mask, scalars, k0, k1, k2, out):
    f32, f16, u8, i32 = mybir.dt.float32, mybir.dt.float16, mybir.dt.uint8, mybir.dt.int32
    ALU, ACT, AX = mybir.AluOpType, mybir.ActivationFunctionType, mybir.AxisListType

    x_rows = x.rearrange("(c p t) d -> p c t d", c=NC, p=P)
    out_rows = out.rearrange("(c p t) d -> p c t d", c=NC, p=P)

    ctx = ExitStack()
    with ctx:
        def sb(name, shape, dt=f32):
            return ctx.enter_context(nc.sbuf_tensor(name, shape, dt))

        def sem(name):
            return ctx.enter_context(nc.semaphore(name))

        x_sb = sb("x_sb", [P, NC, T, D])
        xT_sb = sb("xT_sb", [P, KD, CHUNK])
        ctxT_sb = sb("ctxT_sb", [P, KD, BL])
        wkT_sb = sb("wkT_sb", [P, KD, D])
        wvT_sb = sb("wvT_sb", [P, KD, D])
        wq_sb = sb("wq_sb", [P, KD, D])
        wfcT_sb = sb("wfcT_sb", [P, KD, D])
        cols = sb("cols", [P, 6])
        bfc_sb = sb("bfc_sb", [L, D])
        mask_sb = sb("mask_sb", [P, BL], u8)
        scal = sb("scal", [P, 5])
        k0_sb = sb("k0_sb", [P, 2 * KD, H], u8)
        k1_sb = sb("k1_sb", [P, KH, H], u8)
        k2_sb = sb("k2_sb", [P, KH, D], u8)

        W0 = sb("W0", [P, KD, H], f16)
        W0_top = sb("W0_top", [P, KD, H], f16)
        W0_bottom = sb("W0_bottom", [P, KD, H], f16)
        W1 = sb("W1", [P, KH, H], f16)
        W2 = sb("W2", [P, KH, D], f16)

        ident = sb("ident", [P, P])
        ones = sb("ones", [P, P])
        wq_mean = sb("wq_mean", [P, 2, KD])
        wqc = sb("wqc", [P, KD, D])
        bq_wide = sb("bq_wide", [P, KD, P])
        KT = sb("KT", [P, B, KD, L])
        VT = sb("VT", [P, B, KD, L])
        warm_up = sb("warm_up", [P, 512], f16)
        G = sb("G", [P, KD, NC, L])
        key_bias = sb("key_bias", [P, NC, L])
        V2 = sb("V2", [L, NC, D])
        gates = sb("gates", [P, 2])
        gate_x = sb("gate_x", [P, NC])
        all_masked = sb("all_masked", [P, 4, B])
        signs = sb("signs", [P, 3, 2])
        weight_scale = sb("weight_scale", [P, 5])
        out_gate = sb("out_gate", [P, 3])

        stats = sb("stats", [P, T, 6])
        mean_var = sb("mean_var", [P, T, 2])
        var_eps = sb("var_eps", [P, T])
        std = sb("std", [P, T])
        rstd_guess = sb("rstd_guess", [P, T])
        newton = sb("newton", [P, 2, T])
        wait_bearer = sb("wait_bearer", [P, 1])
        rstd_q = sb("rstd_q", [P, T])
        scores = sb("scores", [P, T, L])
        neg_max = sb("neg_max", [P, T])
        probs = sb("probs", [P, T, L])
        prob_sum = sb("prob_sum", [P, T])
        row_scale = sb("row_scale", [P, 2, T])
        rstd_n = sb("rstd_n", [P, T])
        probsT = sb("probsT", [L, CHUNK])
        xn = sb("xn", [P, T, D])

        nT = [sb(f"nT_{h}", [P, KD, CHUNK], f16) for h in ("hi", "lo")]
        h1 = [sb(f"h1_{h}", [P, KH, CHUNK], f16) for h in ("hi", "lo")]
        h2 = [sb(f"h2_{h}", [P, KH, CHUNK], f16) for h in ("hi", "lo")]

        hid = [ctx.enter_context(nc.psum_tensor(f"hid{i}", [P, 512], f32)) for i in range(NF)]
        aux = [ctx.enter_context(nc.psum_tensor(f"aux{i}", [P, 512], f32)) for i in range(4)]
        ps_K, ps_V, ps_G = (h[:, 0:L * KD].rearrange("p (a b) -> p a b", a=KD) for h in hid[0:3])
        ps_qb, ps_V2 = hid[3][:, 0:L], aux[2][0:L, 0:D]
        ps_scores = aux[0][:, 0:T * L].rearrange("p (t l) -> p t l", t=T)
        ps_probsT = [aux[1], aux[0]]
        ps_nT = [aux[h][:, :].rearrange("p (k n) -> p k n", k=KD) for h in range(HALVES)]
        ps_rows = [aux[2 + t // TB][:, (t % TB) * D:(t % TB + 1) * D] for t in range(T)]

        ctx_in, wk_in, wv_in, wq_in, wfc_in = sem("ctx_in"), sem("wk_in"), sem("wv_in"), sem("wq_in"), sem("wfc_in")
        cols_in, scal_in, mask_in, bfc_in = sem("cols_in"), sem("scal_in"), sem("mask_in"), sem("bfc_in")
        x_in = [sem(f"x_in{c}") for c in range(NC)]
        xT_in = sem("xT_in")
        k0_in, k1_in, k2_in = sem("k0_in"), [sem(f"k1_in{i}") for i in range(2)], sem("k2_in")
        ident_step = sem("ident_step")
        ones_set, warm_up_set = sem("ones_set"), sem("warm_up_set")
        setup_step = sem("setup_step")
        wqc_done, bq_wide_done = sem("wqc_done"), sem("bq_wide_done")
        K_mm, G_mm, qb_mm, V_mm, V2_mm = sem("K_mm"), sem("G_mm"), sem("qb_mm"), sem("V_mm"), sem("V2_mm")
        key_bias_done = sem("key_bias_done")
        KT_done, VT_done, G_done, V2_done = sem("KT_done"), sem("VT_done"), sem("G_done"), sem("V2_done")
        gates_done, weight_scale_done = sem("gates_done"), sem("weight_scale_done")
        W1_by_act_done = sem("W1_by_act_done")
        W0_parts_done, W0_done, W1_done, W2_done = (sem("W0_parts_done"), sem("W0_done"),
                                                     sem("W1_done"), sem("W2_done"))
        attend_step = sem("attend_step")
        std_done = sem("std_done")
        scores_mm, neg_max_done, probs_done = sem("scores_mm"), sem("neg_max_done"), sem("probs_done")
        probsT_mm, probsT_done, values_mm = sem("probsT_mm"), sem("probsT_done"), sem("values_mm")
        xn_done, nT_mm, nT_hi_done, nT_lo_done = (sem("xn_done"), sem("nT_mm"), sem("nT_hi_done"),
                                                  sem("nT_lo_done"))
        hidden_mm, hi_done, lo_done = sem("hidden_mm"), sem("hi_done"), sem("lo_done")
        rows_mm, rows_done = sem("rows_mm"), sem("rows_done")
        stored = sem("stored")

        block = ctx.enter_context(nc.Block())

        def at(tensor, c):
            return tensor[:, c] if isinstance(c, int) else tensor[:, bass.ds(c, 1)]

        @block.sync
        def _(sp):
            sp.dma_start(wq_sb[:], wq).then_inc(wq_in, 16)
            sp.dma_start(ctxT_sb[:], ctxT).then_inc(ctx_in, 16)
            sp.dma_start(wkT_sb[:], wkT).then_inc(wk_in, 16)
            sp.dma_start(wvT_sb[:], wvT).then_inc(wv_in, 16)
            sp.dma_start(x_sb[:, 0], x_rows[:, 0]).then_inc(x_in[0], 16)
            sp.dma_start(xT_sb[:], xT[:, 0]).then_inc(xT_in, 16)
            sp.dma_start(wfcT_sb[:], wfcT).then_inc(wfc_in, 16)
            sp.dma_start(k0_sb[:], k0).then_inc(k0_in, 16)
            for i in range(2):
                part = slice(i * KH // 2, (i + 1) * KH // 2)
                sp.dma_start(k1_sb[:, part], k1[:, part]).then_inc(k1_in[i], 16)
            sp.dma_start(k2_sb[:], k2).then_inc(k2_in, 16)
            for c in range(1, NC):
                sp.dma_start(x_sb[:, c], x_rows[:, c]).then_inc(x_in[c], 16)
            with sp.Fori(0, NC - 1) as c:
                sp.wait_ge(scores_mm, c + 1)
                sp.dma_start(xT_sb[:], xT[:, bass.ds(c + 1, 1)]).then_inc(xT_in, 16)
                sp.wait_ge(rows_done, T * c + T)
                sp.dma_start(out_rows[:, bass.ds(c, 1)], x_sb[:, bass.ds(c, 1)]).then_inc(stored, 16)
            for t in range(T):
                sp.wait_ge(rows_done, T * (NC - 1) + t + 1)
                sp.dma_start(out_rows[:, NC - 1, t], x_sb[:, NC - 1, t]).then_inc(stored, 16)
            sp.wait_ge(stored, 16 * (NC - 1 + T))

        @block.gpsimd
        def _(pool):
            nc.gpsimd.memset(warm_up[:], 0.0).then_inc(warm_up_set, 1)
            pool.dma_start(mask_sb[:], mask.partition_broadcast(P)).then_inc(mask_in, 16)
            pool.dma_start(bfc_sb[:], bfc.partition_broadcast(L)).then_inc(bfc_in, 16)
            nc.gpsimd.memset(ones[:], 1.0).then_inc(ones_set, 1)
            nc.gpsimd.memset(ident[:], 0.0).then_inc(ident_step, 1)
            pool.wait_ge(ident_step, 1)
            nc.gpsimd.affine_select(out=ident[:], in_=ident[:], compare_op=ALU.not_equal, fill=1.0, base=0,
                                    pattern=[[-1, P]], channel_multiplier=1).then_inc(ident_step, 1)
            pool.wait_ge(weight_scale_done, 1)
            pool.wait_ge(k0_in, 16)
            for i, part in enumerate((W0_top, W0_bottom)):
                nc.gpsimd.tensor_scalar(part[:], k0_sb[:, i * KD:(i + 1) * KD], weight_scale[:, i:i + 1], 0.0,
                                        ALU.mult, ALU.add).then_inc(W0_parts_done, 1)
            pool.wait_ge(W0_parts_done, 2)
            nc.gpsimd.tensor_tensor(W0[:], W0_top[:], W0_bottom[:], ALU.add).then_inc(W0_done, 1)
            for k in range(W1_BY_ACT, KH):
                if k in (W1_BY_ACT, KH // 2):
                    pool.wait_ge(k1_in[k // (KH // 2)], 16)
                nc.gpsimd.tensor_scalar(W1[:, k], k1_sb[:, k], weight_scale[:, 2:3], weight_scale[:, 3:4],
                                        ALU.mult, ALU.add).then_inc(W1_done, 1)
            pool.wait_ge(k2_in, 16)
            nc.gpsimd.tensor_scalar(W2[:], k2_sb[:], 2.0, -1.0, ALU.mult, ALU.add).then_inc(W2_done, 1)

        @block.scalar
        def _(act):
            act.dma_start(cols[:], bias_cols).then_inc(cols_in, 16)
            act.dma_start(scal[:], scalars.partition_broadcast(P)).then_inc(scal_in, 16)
            act.preload_act_table(ACT.Sqrt)

            def root(c, which):
                act.wait_ge(attend_step, ATTEND_STEPS * c + (3 if which == 0 else ATTEND_STEPS - RSTD_STEPS + 1))
                nc.scalar.activation(std[:], var_eps[:], ACT.Sqrt).then_inc(std_done, 1)

            def exponentials(c):
                for t in range(T):
                    if t % TB == 0:
                        act.wait_ge(neg_max_done, HALVES * c + t // TB + 1)
                    nc.scalar.activation(probs[:, t], scores[:, t], ACT.Exp, bias=neg_max[:, t:t + 1], scale=1.0,
                                         accum_out=prob_sum[:, t:t + 1]).then_inc(probs_done, 1)

            def copy_probsT(c):
                for h in range(HALVES):
                    act.wait_ge(probsT_mm, HALVES * c + h + 1)
                    nc.scalar.activation(probsT[:, h * HALF:(h + 1) * HALF], ps_probsT[h][0:L, 0:HALF],
                                         ACT.Copy).then_inc(probsT_done, 1)

            def split_hi(c):
                for h in range(HALVES):
                    act.wait_ge(nT_mm, HALVES * c + h + 1)
                    nc.scalar.activation(nT[0][:, :, h * HALF:(h + 1) * HALF], ps_nT[h], ACT.Copy,
                                         scale=N_SCALE).then_inc(nT_hi_done, 1)

            def mlp(c, attend_next):
                for n in range(HB):
                    h = (h1, h2)[n // KH][0]
                    act.wait_ge(hidden_mm, HB * c + n + 1)
                    nc.scalar.activation(h[:, n % KH], hid[n % NF][:, :], ACT.Relu).then_inc(hi_done, 1)
                    if attend_next and n == 8:
                        root(c + 1, 0)
                    if attend_next and n == 9:
                        exponentials(c + 1)
                    if attend_next and n == 10:
                        copy_probsT(c + 1)
                    if attend_next and n == 12:
                        root(c + 1, 1)
                    if attend_next and n == 14:
                        split_hi(c + 1)

            def evacuate_K(b):
                act.wait_ge(K_mm, b + 1)
                for m in range(KD):
                    nc.scalar.activation(KT[:, b, m], ps_K[:, m], ACT.Identity,
                                         bias=cols[:, m:m + 1]).then_inc(KT_done, 1)

            def evacuate_G(b):
                act.wait_ge(G_mm, b + 1)
                for c in range(b * CB, (b + 1) * CB):
                    nc.scalar.activation(G[:, :, c], ps_G, ACT.Copy).then_inc(G_done, 1)

            def evacuate_V(b):
                act.wait_ge(V_mm, b + 1)
                for m in range(KD):
                    nc.scalar.activation(VT[:, b, m], ps_V[:, m], ACT.Identity,
                                         bias=cols[:, KD + m:KD + m + 1]).then_inc(VT_done, 1)

            def scale_W1(k):
                nc.scalar.activation(W1[:, k], k1_sb[:, k], ACT.Identity, bias=weight_scale[:, 3:4],
                                     scale=weight_scale[:, 2:3]).then_inc(W1_by_act_done, 1)

            act.wait_ge(cols_in, 16)
            evacuate_K(0)
            evacuate_V(0)
            evacuate_G(0)
            root(0, 0)
            act.preload_act_table(ACT.Exp)
            act.wait_ge(weight_scale_done, 1)
            act.wait_ge(k1_in[0], 16)
            for k in range(W1_BY_ACT - 1):
                scale_W1(k)
            exponentials(0)
            act.wait_ge(scal_in, 16)
            nc.scalar.activation(gates[:], scal[:, 0:2], ACT.Tanh).then_inc(gates_done, 1)
            copy_probsT(0)
            act.preload_act_table(ACT.Sqrt)
            scale_W1(W1_BY_ACT - 1)
            evacuate_K(1)
            evacuate_V(1)
            evacuate_G(1)
            root(0, 1)
            split_hi(0)
            with act.Fori(0, NC - 1) as c:
                mlp(c, True)
            mlp(NC - 1, False)

        @block.vector
        def _(dve):
            V = nc.vector

            def row_rstd(c, base, which, dst):
                V.tensor_scalar(var_eps[:], mean_var[:, :, 1], EPS, None, ALU.add).then_inc(attend_step, 1)
                dve.wait_ge(std_done, 2 * c + which + 1)
                V.reciprocal(rstd_guess[:], std[:]).then_inc(attend_step, 1)
                dve.wait_ge(attend_step, base + 2)
                V.tensor_tensor(newton[:, 0], rstd_guess[:], rstd_guess[:], ALU.mult).then_inc(attend_step, 1)
                dve.wait_ge(attend_step, base + 3)
                V.scalar_tensor_tensor(newton[:, 1], newton[:, 0], -0.5, var_eps[:],
                                       ALU.mult, ALU.mult).then_inc(attend_step, 1)
                dve.wait_ge(attend_step, base + 4)
                V.scalar_tensor_tensor(dst, newton[:, 1], 1.5, rstd_guess[:],
                                       ALU.add, ALU.mult).then_inc(attend_step, 1)

            def tile(c, t):
                return x_sb[:, c, t] if isinstance(c, int) else x_sb[:, bass.ds(c, 1), t]

            def statistics(c, base):
                for t in range(T):
                    last = V.bn_stats(stats[:, t], tile(c, t))
                last.then_inc(attend_step, 1)
                dve.wait_ge(attend_step, base + 1)
                V.tensor_copy(wait_bearer[:], scal[:, 0:1])
                for t in range(T):
                    last = V.bn_aggr(mean_var[:, t], stats[:, t])
                last.then_inc(attend_step, 1)
                dve.wait_ge(attend_step, base + 2)

            def query_rstd(c):
                base = ATTEND_STEPS * c
                statistics(c, base)
                row_rstd(c, base + 2, 0, rstd_q[:])

            def softmax_max(c):
                base = ATTEND_STEPS * c + 2 + RSTD_STEPS
                dve.wait_ge(attend_step, base)
                dve.wait_ge(scores_mm, c + 1)
                for h in range(HALVES):
                    tiles = range(h * TB, (h + 1) * TB)
                    for t in tiles:
                        last = V.scalar_tensor_tensor(scores[:, t], ps_scores[:, t], rstd_q[:, t:t + 1],
                                                      at(key_bias, c), ALU.mult, ALU.add)
                    last.then_inc(attend_step, 1)
                    dve.wait_ge(attend_step, base + h + 1)
                    V.reduce_max(neg_max[:, tiles[0]:tiles[-1] + 1], scores[:, tiles[0]:tiles[-1] + 1], AX.X,
                                 negate=True).then_inc(neg_max_done, 1)

            def residual_and_norm(c):
                base = ATTEND_STEPS * c + 2 + RSTD_STEPS + HALVES
                dve.wait_ge(probs_done, T * c + T)
                V.reciprocal(row_scale[:, 0], prob_sum[:]).then_inc(attend_step, 1)
                dve.wait_ge(attend_step, base + 1)
                V.tensor_scalar(row_scale[:, 1], row_scale[:, 0], gate_x[:, bass.ds(c, 1)], None,
                                ALU.mult).then_inc(attend_step, 1)
                dve.wait_ge(attend_step, base + 2)
                for t in range(T):
                    if t % TB == 0:
                        dve.wait_ge(values_mm, HALVES * c + t // TB + 1)
                    last = V.scalar_tensor_tensor(tile(c, t), ps_rows[t], row_scale[:, 1, t:t + 1], tile(c, t),
                                                  ALU.mult, ALU.add)
                last.then_inc(attend_step, 1)
                dve.wait_ge(attend_step, base + 3)
                V.tensor_copy(wait_bearer[:], scal[:, 0:1])
                statistics(c, base + 3)
                row_rstd(c, base + 5, 1, rstd_n[:])
                dve.wait_ge(attend_step, base + 5 + RSTD_STEPS)
                for t in range(T):
                    V.tensor_scalar(xn[:, t], tile(c, t), mean_var[:, t, 0:1], rstd_n[:, t:t + 1],
                                    ALU.subtract, ALU.mult).then_inc(xn_done, 1)

            def split_lo(c):
                for h in range(HALVES):
                    cols_h = slice(h * HALF, (h + 1) * HALF)
                    dve.wait_ge(nT_hi_done, HALVES * c + h + 1)
                    V.scalar_tensor_tensor(nT[1][:, :, cols_h], ps_nT[h], N_SCALE, nT[0][:, :, cols_h],
                                           ALU.mult, ALU.subtract).then_inc(nT_lo_done, 1)

            def output_rows(c, t, rows):
                V.scalar_tensor_tensor(tile(c, t), rows, out_gate[:, 2:3], tile(c, t),
                                       ALU.mult, ALU.add).then_inc(rows_done, 1)

            def mlp(c, attend_next):
                for n in range(HB):
                    hi, lo = (h1, h2)[n // KH]
                    dve.wait_ge(hi_done, HB * c + n + 1)
                    V.scalar_tensor_tensor(lo[:, n % KH], hid[n % NF][:, :], 0.0, hi[:, n % KH],
                                           ALU.max, ALU.subtract).then_inc(lo_done, 1)
                    if attend_next and n == 8:
                        query_rstd(c + 1)
                        softmax_max(c + 1)
                    if attend_next and n == 11:
                        residual_and_norm(c + 1)
                    if attend_next and n == 14:
                        split_lo(c + 1)
                for t in range(T):
                    if attend_next:
                        if t % TB == 0:
                            dve.wait_ge(rows_mm, HALVES * c + t // TB + 1)
                        output_rows(c, t, ps_rows[t])
                    else:
                        dve.wait_ge(rows_mm, HALVES * (NC - 1) + t + 1)
                        output_rows(c, t, hid[t][:, 0:D])

            dve.wait_ge(scal_in, 16)
            V.tensor_scalar(signs[:, 0], scal[:, 2:4], 0.0, None, ALU.is_lt).then_inc(setup_step, 1)
            dve.wait_ge(setup_step, 1)
            V.scalar_tensor_tensor(signs[:, 1], scal[:, 2:4], 0.0, signs[:, 0],
                                   ALU.is_gt, ALU.subtract).then_inc(setup_step, 1)
            dve.wait_ge(setup_step, 2)
            V.tensor_scalar(weight_scale[:, 0:1], signs[:, 1, 0:1], 2 * W0_SCALE, None, ALU.mult)
            V.tensor_scalar(weight_scale[:, 1:2], signs[:, 1, 0:1], -2 * W0_SCALE, None, ALU.mult)
            V.tensor_scalar(weight_scale[:, 2:3], signs[:, 1, 1:2], 2 * W1_SCALE, None, ALU.mult)
            V.tensor_scalar(weight_scale[:, 3:4], signs[:, 1, 1:2], -W1_SCALE, None,
                            ALU.mult).then_inc(weight_scale_done, 1)

            dve.wait_ge(wq_in, 16)
            V.reduce_sum(wq_mean[:, 0], wq_sb[:], AX.X).then_inc(setup_step, 1)
            dve.wait_ge(setup_step, 3)
            V.tensor_scalar(wq_mean[:, 1], wq_mean[:, 0], -1.0 / D, None, ALU.mult).then_inc(setup_step, 1)
            dve.wait_ge(setup_step, 4)
            for k in range(KD):
                V.tensor_scalar(wqc[:, k], wq_sb[:, k], wq_mean[:, 1, k:k + 1], None,
                                ALU.add).then_inc(wqc_done, 1)
            dve.wait_ge(cols_in, 16)
            dve.wait_ge(ones_set, 1)
            for k in range(KD):
                V.tensor_scalar(bq_wide[:, k], ones[:], cols[:, 2 * KD + k:2 * KD + k + 1], None,
                                ALU.mult).then_inc(bq_wide_done, 1)

            dve.wait_ge(x_in[0], 16)
            query_rstd(0)

            def add_mask(b):
                dve.wait_ge(qb_mm, b + 1)
                for c in range(b * CB, (b + 1) * CB):
                    V.scalar_tensor_tensor(key_bias[:, c], mask_sb[:, b * L:(b + 1) * L], MASKED, ps_qb,
                                           ALU.mult, ALU.add).then_inc(key_bias_done, 1)

            def evacuate_V2(b):
                dve.wait_ge(V2_mm, b + 1)
                for c in range(b * CB, (b + 1) * CB):
                    V.tensor_tensor(V2[:, c], ps_V2, bfc_sb[:], ALU.add).then_inc(V2_done, 1)

            dve.wait_ge(mask_in, 16)
            add_mask(0)
            dve.wait_ge(key_bias_done, CB)
            softmax_max(0)
            dve.wait_ge(bfc_in, 16)
            evacuate_V2(0)
            V.tensor_tensor(signs[:, 2], signs[:, 1], scal[:, 2:4], ALU.mult).then_inc(setup_step, 1)
            V.tensor_reduce(all_masked[:, 0], mask_sb[:].rearrange("p (b l) -> p b l", b=B), AX.X,
                            ALU.min).then_inc(setup_step, 1)
            dve.wait_ge(setup_step, 6)
            V.scalar_tensor_tensor(out_gate[:, 0:1], signs[:, 2, 0:1], OUT_SCALE, signs[:, 2, 1:2],
                                   ALU.mult, ALU.mult).then_inc(setup_step, 1)
            V.tensor_scalar(all_masked[:, 1], all_masked[:, 0], -1.0, 1.0, ALU.mult, ALU.add).then_inc(setup_step, 1)
            dve.wait_ge(setup_step, 8)
            V.tensor_tensor(out_gate[:, 1:2], out_gate[:, 0:1], scal[:, 4:5], ALU.mult).then_inc(setup_step, 1)
            V.reciprocal(all_masked[:, 2], all_masked[:, 1]).then_inc(setup_step, 1)
            dve.wait_ge(setup_step, 10)
            V.tensor_tensor(all_masked[:, 3], all_masked[:, 2], all_masked[:, 2], ALU.subtract).then_inc(setup_step, 1)
            dve.wait_ge(gates_done, 1)
            V.tensor_tensor(out_gate[:, 2:3], out_gate[:, 1:2], gates[:, 1:2], ALU.mult)
            dve.wait_ge(setup_step, 11)
            for c in range(NC):
                last = V.tensor_tensor(gate_x[:, c:c + 1], all_masked[:, 3, c // CB:c // CB + 1], gates[:, 0:1],
                                       ALU.add)
            last.then_inc(setup_step, 1)
            dve.wait_ge(setup_step, 12)
            residual_and_norm(0)
            add_mask(1)
            evacuate_V2(1)
            split_lo(0)
            for c in range(1, NC):
                dve.wait_ge(x_in[c], 16)
            dve.wait_ge(key_bias_done, NC)
            with dve.Fori(0, NC - 1) as c:
                mlp(c, True)
            mlp(NC - 1, False)

        @block.tensor
        def _(pe):
            def query_scores(c):
                pe.wait_ge(xT_in, 16 * c + 16)
                for t in range(T):
                    for k in range(KD):
                        g = G[:, k, c] if isinstance(c, int) else G[:, k, bass.ds(c, 1)]
                        last = nc.tensor.matmul(ps_scores[:, t], xT_sb[:, k, t * P:(t + 1) * P], g,
                                                start=(k == 0), stop=(k == KD - 1))
                last.then_inc(scores_mm, 1)

            def transpose_probs(c):
                for t in range(T):
                    h, i = t // TB, t % TB
                    pe.wait_ge(probs_done, T * c + t + 1)
                    last = nc.tensor.transpose(ps_probsT[h][0:L, i * P:(i + 1) * P], probs[:, t], ident[:])
                    if i == TB - 1:
                        last.then_inc(probsT_mm, 1)

            def attend_values(c):
                for t in range(T):
                    if t % TB == 0:
                        pe.wait_ge(probsT_done, HALVES * c + t // TB + 1)
                    last = nc.tensor.matmul(ps_rows[t][:, :], probsT[:, t * P:(t + 1) * P], at(V2, c),
                                            start=True, stop=True)
                    if t % TB == TB - 1:
                        last.then_inc(values_mm, 1)

            def transpose_xn(c):
                for h in range(HALVES):
                    pe.wait_ge(xn_done, T * c + TB * (h + 1))
                    for k in range(KD):
                        for i in range(TB):
                            last = nc.tensor.transpose(ps_nT[h][:, k, i * P:(i + 1) * P],
                                                       xn[:, h * TB + i, k * P:(k + 1) * P], ident[:])
                    last.then_inc(nT_mm, 1)

            def mlp(c, attend_next):
                for m in range(KH):
                    if m >= NF:
                        pe.wait_ge(lo_done, HB * c + m - NF + 1)
                    for part, ready in enumerate((nT_hi_done, nT_lo_done)):
                        if m == 0:
                            pe.wait_ge(ready, HALVES * c + HALVES)
                        for k in range(KD):
                            last = nc.tensor.matmul(hid[m % NF][:, :], W0[:, k, m * P:(m + 1) * P], nT[part][:, k],
                                                    start=(k == 0 and part == 0), stop=(k == KD - 1 and part == 1))
                    last.then_inc(hidden_mm, 1)
                pe.wait_ge(W1_by_act_done, W1_BY_ACT)
                pe.wait_ge(W1_done, KH - W1_BY_ACT)
                for m in range(KH):
                    if attend_next and m == 1:
                        query_scores(c + 1)
                    if attend_next and m == 3:
                        transpose_probs(c + 1)
                    if attend_next and m == 4:
                        attend_values(c + 1)
                    if attend_next and m == 7:
                        transpose_xn(c + 1)
                    pe.wait_ge(lo_done, HB * c + KH + m - NF + 1)
                    for part, ready in enumerate((hi_done, lo_done)):
                        for k in range(KH):
                            if m == 0:
                                pe.wait_ge(ready, HB * c + k + 1)
                            last = nc.tensor.matmul(hid[m % NF][:, :], W1[:, k, m * P:(m + 1) * P], h1[part][:, k],
                                                    start=(k == 0 and part == 0), stop=(k == KH - 1 and part == 1))
                    last.then_inc(hidden_mm, 1)
                pe.wait_ge(W2_done, 1)
                if not attend_next:
                    pe.wait_ge(lo_done, HB * c + HB - NF + 1)
                for t in range(T):
                    rows = ps_rows[t] if attend_next else hid[t][:, 0:D]
                    for part, ready in enumerate((hi_done, lo_done)):
                        for k in range(KH):
                            if t == 0:
                                pe.wait_ge(ready, HB * c + KH + k + 1)
                            last = nc.tensor.matmul(rows, h2[part][:, k, t * P:(t + 1) * P], W2[:, k],
                                                    start=(k == 0 and part == 0), stop=(k == KH - 1 and part == 1))
                    if not attend_next or t % TB == TB - 1:
                        last.then_inc(rows_mm, 1)

            def product(dst, lhsT, rhs):
                for k in range(KD):
                    last = nc.tensor.matmul(dst, lhsT(k), rhs(k), start=(k == 0), stop=(k == KD - 1))
                return last

            def project_K(b):
                for m in range(KD):
                    last = product(ps_K[:, m], lambda k: wkT_sb[:, k, m * P:(m + 1) * P],
                                   lambda k: ctxT_sb[:, k, b * L:(b + 1) * L])
                last.then_inc(K_mm, 1)

            def project_V(b):
                for m in range(KD):
                    last = product(ps_V[:, m], lambda k: wvT_sb[:, k, m * P:(m + 1) * P],
                                   lambda k: ctxT_sb[:, k, b * L:(b + 1) * L])
                last.then_inc(V_mm, 1)

            def fold_keys(b):
                pe.wait_ge(KT_done, KD * (b + 1))
                for m in range(KD):
                    last = product(ps_G[:, m], lambda k: wqc[:, k, m * P:(m + 1) * P], lambda k: KT[:, b, k])
                last.then_inc(G_mm, 1)
                product(ps_qb, lambda k: bq_wide[:, k], lambda k: KT[:, b, k]).then_inc(qb_mm, 1)

            def fold_values(b):
                pe.wait_ge(VT_done, KD * (b + 1))
                product(ps_V2, lambda k: VT[:, b, k], lambda k: wfcT_sb[:, k]).then_inc(V2_mm, 1)

            pe.wait_ge(warm_up_set, 1)
            for _ in range(WARM_UP):
                nc.tensor.matmul(hid[3][:, :], warm_up[:, 0:P], warm_up[:], start=True, stop=True)

            pe.wait_ge(ctx_in, 16)
            pe.wait_ge(wk_in, 16)
            project_K(0)
            pe.wait_ge(wv_in, 16)
            project_V(0)
            pe.wait_ge(wqc_done, KD)
            pe.wait_ge(bq_wide_done, KD)
            fold_keys(0)
            pe.wait_ge(G_done, 1)
            query_scores(0)
            pe.wait_ge(wfc_in, 16)
            fold_values(0)
            pe.wait_ge(ident_step, 2)
            transpose_probs(0)
            pe.wait_ge(V2_done, CB)
            attend_values(0)
            project_K(1)
            project_V(1)
            pe.wait_ge(G_done, CB)
            pe.wait_ge(key_bias_done, CB)
            fold_keys(1)
            pe.wait_ge(attend_step, X1_STEP)
            fold_values(1)
            transpose_xn(0)
            pe.wait_ge(key_bias_done, NC)
            pe.wait_ge(V2_done, NC)
            pe.wait_ge(G_done, NC)
            pe.wait_ge(W0_done, 1)
            with pe.Fori(0, NC - 1) as c:
                mlp(c, True)
            mlp(NC - 1, False)


def kernel(**inputs):
    import concourse.bacc as bacc
    from concourse.bass_utils import run_bass_kernel_spmd

    a = {name: np.asarray(v) for name, v in inputs.items()}

    def tiles(m):
        return np.ascontiguousarray(m.reshape(m.shape[0] // P, P, m.shape[1]).transpose(1, 0, 2))

    x = a["x"].reshape(B * S, D)
    arrays = {
        "x": x,
        "xT": x.reshape(NC, P, T, KD, P).transpose(4, 0, 3, 2, 1).reshape(P, NC, KD, CHUNK),
        "ctxT": tiles(a["ctx_1024"].reshape(BL, D).T),
        "wkT": tiles(a["L0_xattn_Wk"][:D].T),
        "wvT": tiles(a["L0_xattn_Wk"][D:].T),
        "wq": tiles(a["L0_xattn_Wq"]),
        "wfcT": tiles(a["L0_xattn_Wfc"].T),
        "bias_cols": np.concatenate([a["L0_xattn_bk"].reshape(-1, P).T, a["L0_xattn_bq"].reshape(-1, P).T], 1),
        "bfc": a["L0_xattn_bfc"],
        "mask": a["mask_BxS2_bk0"].reshape(BL),
        "scalars": np.concatenate([a[n].reshape(1) for n in
                                   ("g_xattn", "g_ffn", "L0_ffn_s0", "L0_ffn_s1", "L0_ffn_s2")]),
        "k0": tiles(a["L0_ffn_k0"]),
        "k1": tiles(a["L0_ffn_k1"]),
        "k2": tiles(a["L0_ffn_k2"]),
    }
    arrays = {n: np.ascontiguousarray(v) for n, v in arrays.items()}
    nc = bacc.Bacc("TRN2", target_bir_lowering=False, num_devices=1)
    args = [nc.dram_tensor(n, v.shape, mybir.dt.from_np(v.dtype), kind="ExternalInput").ap()
            for n, v in arrays.items()]
    out = nc.dram_tensor("out", (B * S, D), mybir.dt.float32, kind="ExternalOutput").ap()
    flamingo_kernel(nc, *args, out)
    r = run_bass_kernel_spmd(nc, [arrays], core_ids=[0])
    return r.results[0]["out"].reshape(B, S, D)
```

```python
from contextlib import ExitStack

import numpy as np

import concourse.bass as bass
from concourse import mybir

P = 128
B, S, D, L, H = 2, 1024, 256, 77, 1024
CHUNK = 512
NC = B * S // CHUNK
CB = S // CHUNK
T = CHUNK // P
KD = D // P
KH = H // P
BL = B * L
HB = 2 * KH
TB = 512 // D
HALVES = T // TB
HALF = CHUNK // HALVES
W1_BY_ACT = 3
WARM_UP = 8
NF = 4

N_SCALE = 2.0 ** 10
W0_SCALE = 2.0 ** -4
W1_SCALE = 2.0 ** -10
OUT_SCALE = 4.0 / (N_SCALE * W0_SCALE * W1_SCALE)
MASKED = -1e30
EPS = 1e-5
STAT_STEPS = 2
RSTD_STEPS = 5
QUERY_STEPS = STAT_STEPS + RSTD_STEPS
NORM_STEPS = 4 + STAT_STEPS + RSTD_STEPS
X1_STEP = 4


def flamingo_kernel(nc, x, xT, ctxT, wkT, wvT, wq, wfcT, bias_cols, bfc, mask, scalars, k0, k1, k2, out):
    f32, f16, u8, i32 = mybir.dt.float32, mybir.dt.float16, mybir.dt.uint8, mybir.dt.int32
    ALU, ACT, AX = mybir.AluOpType, mybir.ActivationFunctionType, mybir.AxisListType

    x_rows = x.rearrange("(c p t) d -> p c t d", c=NC, p=P)
    out_rows = out.rearrange("(c p t) d -> p c t d", c=NC, p=P)

    ctx = ExitStack()
    with ctx:
        def sb(name, shape, dt=f32):
            return ctx.enter_context(nc.sbuf_tensor(name, shape, dt))

        def sem(name):
            return ctx.enter_context(nc.semaphore(name))

        x_sb = sb("x_sb", [P, NC, T, D])
        xT_sb = sb("xT_sb", [P, HALVES, KD, HALF])
        ctxT_sb = sb("ctxT_sb", [P, KD, BL])
        wkT_sb = sb("wkT_sb", [P, KD, D])
        wvT_sb = sb("wvT_sb", [P, KD, D])
        wq_sb = sb("wq_sb", [P, KD, D])
        wfcT_sb = sb("wfcT_sb", [P, KD, D])
        cols = sb("cols", [P, 6])
        bfc_sb = sb("bfc_sb", [L, D])
        mask_sb = sb("mask_sb", [P, BL], u8)
        scal = sb("scal", [P, 5])
        k0_sb = sb("k0_sb", [P, 2 * KD, H], u8)
        k1_sb = sb("k1_sb", [P, KH, H], u8)
        k2_sb = sb("k2_sb", [P, KH, D], u8)

        W0 = sb("W0", [P, KD, H], f16)
        W0_top = sb("W0_top", [P, KD, H], f16)
        W0_bottom = sb("W0_bottom", [P, KD, H], f16)
        W1 = sb("W1", [P, KH, H], f16)
        W2 = sb("W2", [P, KH, D], f16)

        ident = sb("ident", [P, P])
        ones = sb("ones", [P, P])
        wq_mean = sb("wq_mean", [P, 2, KD])
        wqc = sb("wqc", [P, KD, D])
        bq_wide = sb("bq_wide", [P, KD, P])
        KT = sb("KT", [P, B, KD, L])
        VT = sb("VT", [P, B, KD, L])
        warm_up = sb("warm_up", [P, 512], f16)
        G = sb("G", [P, KD, NC, L])
        key_bias = sb("key_bias", [P, NC, L])
        V2 = sb("V2", [L, NC, D])
        gates = sb("gates", [P, 2])
        gate_x = sb("gate_x", [P, NC])
        all_masked = sb("all_masked", [P, 4, B])
        signs = sb("signs", [P, 3, 2])
        weight_scale = sb("weight_scale", [P, 5])
        out_gate = sb("out_gate", [P, 3])

        class Rows:

            def __init__(self, name, n):
                self.stats = sb(f"{name}_stats", [P, n, 6])
                self.mean_var = sb(f"{name}_mean_var", [P, n, 2])
                self.var_eps = sb(f"{name}_var_eps", [P, n])
                self.std = sb(f"{name}_std", [P, n])
                self.guess = sb(f"{name}_guess", [P, n])
                self.newton = sb(f"{name}_newton", [P, 2, n])
                self.rstd = sb(f"{name}_rstd", [P, n])
                self.wait_bearer = sb(f"{name}_wait_bearer", [P, 2])
                self.step = sem(f"{name}_step")
                self.std_done = sem(f"{name}_std_done")

        queries = [Rows(f"queries{h}", TB) for h in range(HALVES)]
        norms = [Rows(f"norms{h}", TB) for h in range(HALVES)]
        scores = sb("scores", [P, T, L])
        neg_max = sb("neg_max", [P, T])
        probs = sb("probs", [P, T, L])
        prob_sum = sb("prob_sum", [P, T])
        row_scale = sb("row_scale", [P, 2, T])
        probsT = sb("probsT", [L, CHUNK])
        xn = sb("xn", [P, T, D])

        nT = [sb(f"nT_{h}", [P, KD, CHUNK], f16) for h in ("hi", "lo")]
        h1 = [sb(f"h1_{h}", [P, KH, CHUNK], f16) for h in ("hi", "lo")]
        h2 = [sb(f"h2_{h}", [P, KH, CHUNK], f16) for h in ("hi", "lo")]

        hid = [ctx.enter_context(nc.psum_tensor(f"hid{i}", [P, 512], f32)) for i in range(NF)]
        aux = [ctx.enter_context(nc.psum_tensor(f"aux{i}", [P, 512], f32)) for i in range(4)]
        ps_K, ps_G, *ps_V = (h[:, 0:L * KD].rearrange("p (a b) -> p a b", a=KD)
                             for h in (hid[0], hid[2], hid[1], aux[3]))
        ps_qb, ps_V2 = hid[3][:, 0:L], hid[1][0:L, 0:D]
        ps_scores, ps_probsT, ps_rows, ps_nT = ([aux[i], aux[j]] for i, j in ((0, 3), (1, 3), (2, 3), (0, 1)))
        ps_scores = [s[:, 0:TB * L].rearrange("p (t l) -> p t l", t=TB) for s in ps_scores]
        ps_rows = [s[:, :].rearrange("p (t d) -> p t d", t=TB) for s in ps_rows]
        ps_nT = [s[:, :].rearrange("p (k n) -> p k n", k=KD) for s in ps_nT]

        ctx_in, wk_in, wv_in, wq_in, wfc_in = sem("ctx_in"), sem("wk_in"), sem("wv_in"), sem("wq_in"), sem("wfc_in")
        cols_in, scal_in, mask_in, bfc_in = sem("cols_in"), sem("scal_in"), sem("mask_in"), sem("bfc_in")
        x_in = [sem(f"x_in{c}") for c in range(NC)]
        x_in_second = sem("x_in_second")
        xT_in = [sem(f"xT_in{h}") for h in range(HALVES)]
        k0_in, k1_in, k2_in = sem("k0_in"), [sem(f"k1_in{i}") for i in range(2)], sem("k2_in")
        ident_step = sem("ident_step")
        ones_set, warm_up_set = sem("ones_set"), sem("warm_up_set")
        setup_step = sem("setup_step")
        wqc_done, bq_wide_done = sem("wqc_done"), sem("bq_wide_done")
        K_mm, G_mm, qb_mm, V_mm, V2_mm = sem("K_mm"), sem("G_mm"), sem("qb_mm"), sem("V_mm"), sem("V2_mm")
        key_bias_done = sem("key_bias_done")
        KT_done, VT_done, G_done, V2_done = sem("KT_done"), sem("VT_done"), sem("G_done"), sem("V2_done")
        gates_done, weight_scale_done = sem("gates_done"), sem("weight_scale_done")
        W1_by_act_done = sem("W1_by_act_done")
        W0_parts_done, W0_done, W1_done, W2_done = (sem("W0_parts_done"), sem("W0_done"),
                                                     sem("W1_done"), sem("W2_done"))
        def half_sems(name):
            return [sem(f"{name}{h}") for h in range(HALVES)]

        scores_mm, neg_max_done, probs_done = map(half_sems, ("scores_mm", "neg_max_done", "probs_done"))
        probsT_mm, probsT_done, values_mm = map(half_sems, ("probsT_mm", "probsT_done", "values_mm"))
        xn_done, nT_mm, nT_hi_done, nT_lo_done = map(half_sems, ("xn_done", "nT_mm", "nT_hi_done", "nT_lo_done"))
        hidden_mm, hi_done, lo_done = sem("hidden_mm"), sem("hi_done"), sem("lo_done")
        rows_mm, rows_done = sem("rows_mm"), sem("rows_done")
        stored = sem("stored")

        block = ctx.enter_context(nc.Block())

        both = range(HALVES)

        def tiles_of(h):
            return range(h * TB, (h + 1) * TB)

        def span(h):
            return slice(h * TB, (h + 1) * TB)

        def groups_before(c, part):
            return HB * part if part is not None else HB * c + HB

        def columns(part):
            return slice(0, CHUNK) if part is None else slice(part * HALF, (part + 1) * HALF)

        def at(tensor, c):
            return tensor[:, c] if isinstance(c, int) else tensor[:, bass.ds(c, 1)]

        @block.sync
        def _(sp):
            sp.dma_start(ctxT_sb[:], ctxT).then_inc(ctx_in, 16)
            sp.dma_start(wkT_sb[:], wkT).then_inc(wk_in, 16)
            sp.dma_start(wq_sb[:], wq).then_inc(wq_in, 16)
            sp.dma_start(wvT_sb[:], wvT).then_inc(wv_in, 16)
            sp.dma_start(x_sb[:, 0, span(0)], x_rows[:, 0, span(0)]).then_inc(x_in[0], 16)
            sp.dma_start(xT_sb[:, 0], xT[:, 0, 0]).then_inc(xT_in[0], 16)
            sp.dma_start(wfcT_sb[:], wfcT).then_inc(wfc_in, 16)
            sp.dma_start(k0_sb[:], k0).then_inc(k0_in, 16)
            sp.dma_start(k1_sb[:, 0:KH // 2], k1[:, 0:KH // 2]).then_inc(k1_in[0], 16)
            sp.dma_start(x_sb[:, 0, span(1)], x_rows[:, 0, span(1)]).then_inc(x_in_second, 16)
            sp.dma_start(xT_sb[:, 1], xT[:, 0, 1]).then_inc(xT_in[1], 16)
            sp.dma_start(k1_sb[:, KH // 2:], k1[:, KH // 2:]).then_inc(k1_in[1], 16)
            sp.dma_start(k2_sb[:], k2).then_inc(k2_in, 16)
            for c in range(1, NC):
                sp.dma_start(x_sb[:, c], x_rows[:, c]).then_inc(x_in[c], 16)

            def load_xT(c):
                for h in both:
                    sp.wait_ge(scores_mm[h], c)
                    sp.dma_start(xT_sb[:, h], xT[:, c, h] if isinstance(c, int) else xT[:, bass.ds(c, 1), h])\
                        .then_inc(xT_in[h], 16)

            def store(c):
                sp.wait_ge(rows_done, T * c + T)
                sp.dma_start(at(out_rows, c), at(x_sb, c)).then_inc(stored, 16)

            load_xT(1)
            store(0)
            with sp.Fori(1, NC - 1) as c:
                load_xT(c + 1)
                store(c)
            for t in range(T):
                sp.wait_ge(rows_done, T * (NC - 1) + t + 1)
                sp.dma_start(out_rows[:, NC - 1, t], x_sb[:, NC - 1, t]).then_inc(stored, 16)
            sp.wait_ge(stored, 16 * (NC - 1 + T))

        @block.gpsimd
        def _(pool):
            pool.dma_start(cols[:], bias_cols).then_inc(cols_in, 16)
            pool.dma_start(scal[:], scalars.partition_broadcast(P)).then_inc(scal_in, 16)
            pool.dma_start(mask_sb[:], mask.partition_broadcast(P)).then_inc(mask_in, 16)
            pool.dma_start(bfc_sb[:], bfc.partition_broadcast(L)).then_inc(bfc_in, 16)
            nc.gpsimd.memset(ones[:], 1.0).then_inc(ones_set, 1)
            nc.gpsimd.memset(ident[:], 0.0).then_inc(ident_step, 1)
            pool.wait_ge(ident_step, 1)
            nc.gpsimd.affine_select(out=ident[:], in_=ident[:], compare_op=ALU.not_equal, fill=1.0, base=0,
                                    pattern=[[-1, P]], channel_multiplier=1).then_inc(ident_step, 1)
            pool.wait_ge(cols_in, 16)
            pool.wait_ge(ones_set, 1)
            for k in range(KD):
                nc.gpsimd.tensor_scalar(bq_wide[:, k], ones[:], cols[:, 2 * KD + k:2 * KD + k + 1], 0.0,
                                        ALU.mult, ALU.add).then_inc(bq_wide_done, 1)
            pool.wait_ge(weight_scale_done, 1)
            pool.wait_ge(k0_in, 16)
            for i, part in enumerate((W0_top, W0_bottom)):
                nc.gpsimd.tensor_scalar(part[:], k0_sb[:, i * KD:(i + 1) * KD], weight_scale[:, i:i + 1], 0.0,
                                        ALU.mult, ALU.add).then_inc(W0_parts_done, 1)
            pool.wait_ge(W0_parts_done, 2)
            nc.gpsimd.tensor_tensor(W0[:], W0_top[:], W0_bottom[:], ALU.add).then_inc(W0_done, 1)
            for k in range(W1_BY_ACT, KH):
                if k in (W1_BY_ACT, KH // 2):
                    pool.wait_ge(k1_in[k // (KH // 2)], 16)
                nc.gpsimd.tensor_scalar(W1[:, k], k1_sb[:, k], weight_scale[:, 2:3], weight_scale[:, 3:4],
                                        ALU.mult, ALU.add).then_inc(W1_done, 1)
            pool.wait_ge(k2_in, 16)
            nc.gpsimd.tensor_scalar(W2[:], k2_sb[:], 2.0, -1.0, ALU.mult, ALU.add).then_inc(W2_done, 1)

        @block.scalar
        def _(act):
            act.preload_act_table(ACT.Sqrt)

            def root_queries(c, halves):
                for h in halves:
                    act.wait_ge(queries[h].step, QUERY_STEPS * c + STAT_STEPS + 1)
                    nc.scalar.activation(queries[h].std[:], queries[h].var_eps[:],
                                         ACT.Sqrt).then_inc(queries[h].std_done, 1)

            def root_norms(c, halves):
                for h in halves:
                    act.wait_ge(norms[h].step, NORM_STEPS * (c + 1) - RSTD_STEPS + 1)
                    nc.scalar.activation(norms[h].std[:], norms[h].var_eps[:], ACT.Sqrt).then_inc(norms[h].std_done, 1)

            def exponentials(c, halves):
                for h in halves:
                    act.wait_ge(neg_max_done[h], c + 1)
                    for t in tiles_of(h):
                        nc.scalar.activation(probs[:, t], scores[:, t], ACT.Exp, bias=neg_max[:, t:t + 1], scale=1.0,
                                             accum_out=prob_sum[:, t:t + 1]).then_inc(probs_done[h], 1)

            def copy_probsT(c, halves):
                for h in halves:
                    act.wait_ge(probsT_mm[h], c + 1)
                    nc.scalar.activation(probsT[:, h * HALF:(h + 1) * HALF], ps_probsT[h][0:L, 0:HALF],
                                         ACT.Copy).then_inc(probsT_done[h], 1)

            def split_hi(c, halves):
                for h in halves:
                    act.wait_ge(nT_mm[h], c + 1)
                    nc.scalar.activation(nT[0][:, :, h * HALF:(h + 1) * HALF], ps_nT[h], ACT.Copy,
                                         scale=N_SCALE).then_inc(nT_hi_done[h], 1)

            def mlp(c, part, next_c, halves):
                tokens = columns(part)
                width = tokens.stop - tokens.start
                for n in range(HB):
                    h = (h1, h2)[n // KH][0]
                    act.wait_ge(hidden_mm, groups_before(c, part) + n + 1)
                    nc.scalar.activation(h[:, n % KH, tokens], hid[n % NF][:, 0:width], ACT.Relu).then_inc(hi_done, 1)
                    if halves and part != 1 and n == 6:
                        root_queries(next_c, halves)
                    if halves and n == 7:
                        exponentials(next_c, halves)
                    if halves and n == 9:
                        copy_probsT(next_c, halves)
                    if halves and n == 11:
                        root_norms(next_c, halves)
                    if part == 0 and n == 15:
                        root_queries(c + 1, both)
                if halves:
                    split_hi(next_c, halves)

            def evacuate_K(b):
                act.wait_ge(K_mm, b + 1)
                for m in range(KD):
                    nc.scalar.activation(KT[:, b, m], ps_K[:, m], ACT.Identity,
                                         bias=cols[:, m:m + 1]).then_inc(KT_done, 1)

            def evacuate_G(b):
                act.wait_ge(G_mm, b + 1)
                for c in range(b * CB, (b + 1) * CB):
                    nc.scalar.activation(G[:, :, c], ps_G, ACT.Copy).then_inc(G_done, 1)

            def evacuate_V(b):
                act.wait_ge(V_mm, KD * (b + 1))
                for m in range(KD):
                    nc.scalar.activation(VT[:, b, m], ps_V[b][:, m], ACT.Identity,
                                         bias=cols[:, KD + m:KD + m + 1]).then_inc(VT_done, 1)

            def scale_W1(k):
                nc.scalar.activation(W1[:, k], k1_sb[:, k], ACT.Identity, bias=weight_scale[:, 3:4],
                                     scale=weight_scale[:, 2:3]).then_inc(W1_by_act_done, 1)

            act.wait_ge(cols_in, 16)
            evacuate_K(0)
            root_queries(0, [0])
            evacuate_G(0)
            evacuate_V(0)
            act.preload_act_table(ACT.Exp)
            exponentials(0, [0])
            act.wait_ge(scal_in, 16)
            nc.scalar.activation(gates[:], scal[:, 0:2], ACT.Tanh).then_inc(gates_done, 1)
            copy_probsT(0, [0])
            evacuate_K(1)
            evacuate_V(1)
            act.preload_act_table(ACT.Sqrt)
            act.wait_ge(weight_scale_done, 1)
            act.wait_ge(k1_in[0], 16)
            evacuate_G(1)
            scale_W1(0)
            root_norms(0, [0])
            scale_W1(1)
            split_hi(0, [0])
            for k in range(2, W1_BY_ACT):
                scale_W1(k)
            mlp(0, 0, 0, [1])
            mlp(0, 1, 1, both)
            with act.Fori(1, NC - 1) as c:
                mlp(c, None, c + 1, both)
            mlp(NC - 1, None, None, [])

        @block.vector
        def _(dve):
            V = nc.vector

            def tile(c, t):
                return x_sb[:, c, t] if isinstance(c, int) else x_sb[:, bass.ds(c, 1), t]

            def statistics(c, rows):
                for r, base, tiles in rows:
                    for i, t in enumerate(tiles):
                        last = V.bn_stats(r.stats[:, i], tile(c, t))
                    last.then_inc(r.step, 1)
                for r, base, tiles in rows:
                    dve.wait_ge(r.step, base + 1)
                    V.tensor_copy(r.wait_bearer[:, 1:2], r.stats[:, 0, 0:1])
                    for i, t in enumerate(tiles):
                        last = V.bn_aggr(r.mean_var[:, i], r.stats[:, i])
                    last.then_inc(r.step, 1)

            def variance(c, rows):
                statistics(c, rows)
                for r, base, _ in rows:
                    dve.wait_ge(r.step, base + STAT_STEPS)
                    V.tensor_scalar(r.var_eps[:], r.mean_var[:, :, 1], EPS, None, ALU.add).then_inc(r.step, 1)

            def row_rstd(c, rows):
                for r, base, _ in rows:
                    dve.wait_ge(r.std_done, c + 1)
                    V.reciprocal(r.guess[:], r.std[:]).then_inc(r.step, 1)
                for r, base, _ in rows:
                    dve.wait_ge(r.step, base + STAT_STEPS + 2)
                    V.tensor_tensor(r.newton[:, 0], r.guess[:], r.guess[:], ALU.mult).then_inc(r.step, 1)
                for r, base, _ in rows:
                    dve.wait_ge(r.step, base + STAT_STEPS + 3)
                    V.scalar_tensor_tensor(r.newton[:, 1], r.newton[:, 0], -0.5, r.var_eps[:],
                                           ALU.mult, ALU.mult).then_inc(r.step, 1)
                for r, base, _ in rows:
                    dve.wait_ge(r.step, base + STAT_STEPS + 4)
                    V.scalar_tensor_tensor(r.rstd[:], r.newton[:, 1], 1.5, r.guess[:],
                                           ALU.add, ALU.mult).then_inc(r.step, 1)

            def query_rows(c, halves):
                return [(queries[h], QUERY_STEPS * c, tiles_of(h)) for h in halves]

            def norm_rows(c, halves):
                return [(norms[h], NORM_STEPS * c + X1_STEP, tiles_of(h)) for h in halves]

            def softmax_max(c, halves):
                for h in halves:
                    dve.wait_ge(queries[h].step, QUERY_STEPS * (c + 1))
                    dve.wait_ge(scores_mm[h], c + 1)
                    for t in tiles_of(h):
                        last = V.scalar_tensor_tensor(scores[:, t], ps_scores[h][:, t - h * TB],
                                                      queries[h].rstd[:, t - h * TB:t - h * TB + 1], at(key_bias, c), ALU.mult, ALU.add)
                    last.then_inc(norms[h].step, 1)
                    dve.wait_ge(norms[h].step, NORM_STEPS * c + 1)
                    V.reduce_max(neg_max[:, span(h)], scores[:, span(h)], AX.X, negate=True).then_inc(neg_max_done[h], 1)

            def residual(c, halves):
                base = NORM_STEPS * c
                for h in halves:
                    dve.wait_ge(probs_done[h], TB * c + TB)
                    V.reciprocal(row_scale[:, 0, span(h)], prob_sum[:, span(h)]).then_inc(norms[h].step, 1)
                for h in halves:
                    dve.wait_ge(norms[h].step, base + 2)
                    V.tensor_scalar(row_scale[:, 1, span(h)], row_scale[:, 0, span(h)], gate_x[:, bass.ds(c, 1)],
                                    None, ALU.mult).then_inc(norms[h].step, 1)
                for h in halves:
                    dve.wait_ge(norms[h].step, base + 3)
                    dve.wait_ge(values_mm[h], c + 1)
                    for t in tiles_of(h):
                        last = V.scalar_tensor_tensor(tile(c, t), ps_rows[h][:, t - h * TB], row_scale[:, 1, t:t + 1],
                                                      tile(c, t), ALU.mult, ALU.add)
                    last.then_inc(norms[h].step, 1)
                for h in halves:
                    dve.wait_ge(norms[h].step, base + X1_STEP)
                    V.tensor_copy(norms[h].wait_bearer[:, 0:1], row_scale[:, 1, h * TB:h * TB + 1])
                variance(c, norm_rows(c, halves))

            def normalise(c, halves):
                row_rstd(c, norm_rows(c, halves))
                for h in halves:
                    dve.wait_ge(norms[h].step, NORM_STEPS * (c + 1))
                    for i, t in enumerate(tiles_of(h)):
                        V.tensor_scalar(xn[:, t], tile(c, t), norms[h].mean_var[:, i, 0:1], norms[h].rstd[:, i:i + 1],
                                        ALU.subtract, ALU.mult).then_inc(xn_done[h], 1)

            def split_lo(c, halves):
                for h in halves:
                    tokens = slice(h * HALF, (h + 1) * HALF)
                    dve.wait_ge(nT_hi_done[h], c + 1)
                    V.scalar_tensor_tensor(nT[1][:, :, tokens], ps_nT[h], N_SCALE, nT[0][:, :, tokens],
                                           ALU.mult, ALU.subtract).then_inc(nT_lo_done[h], 1)

            def mlp(c, part, next_c, halves):
                tokens = columns(part)
                width = tokens.stop - tokens.start
                for n in range(HB):
                    hi, lo = (h1, h2)[n // KH]
                    dve.wait_ge(hi_done, groups_before(c, part) + n + 1)
                    V.scalar_tensor_tensor(lo[:, n % KH, tokens], hid[n % NF][:, 0:width], 0.0, hi[:, n % KH, tokens],
                                           ALU.max, ALU.subtract).then_inc(lo_done, 1)
                    if halves and part is None and n == 5:
                        variance(next_c, query_rows(next_c, halves))
                    if halves and n == 7:
                        if part != 1:
                            row_rstd(next_c, query_rows(next_c, halves))
                        softmax_max(next_c, halves)
                    if halves and n == 10:
                        residual(next_c, halves)
                    if halves and n == 12:
                        normalise(next_c, halves)
                    if part == 0 and n == 14:
                        dve.wait_ge(x_in[c + 1], 16)
                        variance(c + 1, query_rows(c + 1, both))
                    if part == 0 and n == 15:
                        row_rstd(c + 1, query_rows(c + 1, both))
                if halves:
                    split_lo(next_c, halves)
                for h in both if part is None else [part]:
                    for i, t in enumerate(tiles_of(h)):
                        if halves:
                            if i == 0:
                                dve.wait_ge(rows_mm, HALVES * c + h + 1)
                            rows = ps_rows[h][:, i]
                        else:
                            dve.wait_ge(rows_mm, HALVES * c + t + 1)
                            rows = hid[t][:, 0:D]
                        V.scalar_tensor_tensor(tile(c, t), rows, out_gate[:, 2:3], tile(c, t),
                                               ALU.mult, ALU.add).then_inc(rows_done, 1)

            V.memset(warm_up[:], 0.0).then_inc(warm_up_set, 1)
            dve.wait_ge(wq_in, 16)
            V.reduce_sum(wq_mean[:, 0], wq_sb[:], AX.X).then_inc(setup_step, 1)
            dve.wait_ge(setup_step, 1)
            V.tensor_scalar(wq_mean[:, 1], wq_mean[:, 0], -1.0 / D, None, ALU.mult).then_inc(setup_step, 1)
            dve.wait_ge(setup_step, 2)
            for k in range(KD):
                V.tensor_scalar(wqc[:, k], wq_sb[:, k], wq_mean[:, 1, k:k + 1], None,
                                ALU.add).then_inc(wqc_done, 1)
            dve.wait_ge(x_in[0], 16)
            variance(0, query_rows(0, [0]))

            dve.wait_ge(scal_in, 16)
            V.tensor_scalar(signs[:, 0], scal[:, 2:4], 0.0, None, ALU.is_lt).then_inc(setup_step, 1)
            dve.wait_ge(setup_step, 3)
            V.scalar_tensor_tensor(signs[:, 1], scal[:, 2:4], 0.0, signs[:, 0],
                                   ALU.is_gt, ALU.subtract).then_inc(setup_step, 1)
            dve.wait_ge(setup_step, 4)
            V.tensor_scalar(weight_scale[:, 0:1], signs[:, 1, 0:1], 2 * W0_SCALE, None, ALU.mult)
            V.tensor_scalar(weight_scale[:, 1:2], signs[:, 1, 0:1], -2 * W0_SCALE, None, ALU.mult)
            V.tensor_scalar(weight_scale[:, 2:3], signs[:, 1, 1:2], 2 * W1_SCALE, None, ALU.mult)
            V.tensor_scalar(weight_scale[:, 3:4], signs[:, 1, 1:2], -W1_SCALE, None,
                            ALU.mult).then_inc(weight_scale_done, 1)

            row_rstd(0, query_rows(0, [0]))

            def chunks_of(b):
                return range(b * CB, (b + 1) * CB)

            def add_mask(c):
                b = c // CB
                dve.wait_ge(qb_mm, b + 1)
                V.scalar_tensor_tensor(key_bias[:, c], mask_sb[:, b * L:(b + 1) * L], MASKED, ps_qb,
                                       ALU.mult, ALU.add).then_inc(key_bias_done, 1)

            def evacuate_V2(c):
                b = c // CB
                dve.wait_ge(V2_mm, b + 1)
                V.tensor_tensor(V2[:, c], ps_V2, bfc_sb[:], ALU.add).then_inc(V2_done, 1)

            dve.wait_ge(mask_in, 16)
            add_mask(0)
            dve.wait_ge(key_bias_done, 1)
            softmax_max(0, [0])
            V.tensor_tensor(signs[:, 2], signs[:, 1], scal[:, 2:4], ALU.mult).then_inc(setup_step, 1)
            V.tensor_reduce(all_masked[:, 0], mask_sb[:].rearrange("p (b l) -> p b l", b=B), AX.X,
                            ALU.min).then_inc(setup_step, 1)
            dve.wait_ge(setup_step, 6)
            V.scalar_tensor_tensor(out_gate[:, 0:1], signs[:, 2, 0:1], OUT_SCALE, signs[:, 2, 1:2],
                                   ALU.mult, ALU.mult).then_inc(setup_step, 1)
            V.tensor_scalar(all_masked[:, 1], all_masked[:, 0], -1.0, 1.0, ALU.mult, ALU.add).then_inc(setup_step, 1)
            dve.wait_ge(setup_step, 8)
            V.tensor_tensor(out_gate[:, 1:2], out_gate[:, 0:1], scal[:, 4:5], ALU.mult).then_inc(setup_step, 1)
            V.reciprocal(all_masked[:, 2], all_masked[:, 1]).then_inc(setup_step, 1)
            dve.wait_ge(setup_step, 10)
            V.tensor_tensor(all_masked[:, 3], all_masked[:, 2], all_masked[:, 2], ALU.subtract).then_inc(setup_step, 1)
            dve.wait_ge(bfc_in, 16)
            evacuate_V2(0)
            dve.wait_ge(gates_done, 1)
            V.tensor_tensor(out_gate[:, 2:3], out_gate[:, 1:2], gates[:, 1:2], ALU.mult)
            dve.wait_ge(setup_step, 11)
            for c in range(NC):
                last = V.tensor_tensor(gate_x[:, c:c + 1], all_masked[:, 3, c // CB:c // CB + 1], gates[:, 0:1],
                                       ALU.add)
            last.then_inc(setup_step, 1)
            dve.wait_ge(setup_step, 12)
            residual(0, [0])
            for c in range(1, CB):
                add_mask(c)
                evacuate_V2(c)
            normalise(0, [0])
            for c in chunks_of(1):
                add_mask(c)
                evacuate_V2(c)
            split_lo(0, [0])
            dve.wait_ge(x_in_second, 16)
            variance(0, query_rows(0, [1]))
            dve.wait_ge(key_bias_done, NC)
            mlp(0, 0, 0, [1])
            mlp(0, 1, 1, both)
            for c in range(2, NC):
                dve.wait_ge(x_in[c], 16)
            with dve.Fori(1, NC - 1) as c:
                mlp(c, None, c + 1, both)
            mlp(NC - 1, None, None, [])

        @block.tensor
        def _(pe):
            def query_score_steps(halves):
                return [(h, i, k) for h in halves for i in range(TB) for k in range(KD)]

            def query_score(c, h, i, k):
                if (i, k) == (0, 0):
                    pe.wait_ge(xT_in[h], 16 * c + 16)
                g = G[:, k, c] if isinstance(c, int) else G[:, k, bass.ds(c, 1)]
                product = nc.tensor.matmul(ps_scores[h][:, i], xT_sb[:, h, k, i * P:(i + 1) * P], g,
                                           start=(k == 0), stop=(k == KD - 1))
                if (i, k) == (TB - 1, KD - 1):
                    product.then_inc(scores_mm[h], 1)

            def transpose_probs(c, halves):
                for h in halves:
                    for i, t in enumerate(tiles_of(h)):
                        pe.wait_ge(probs_done[h], TB * c + i + 1)
                        last = nc.tensor.transpose(ps_probsT[h][0:L, i * P:(i + 1) * P], probs[:, t], ident[:])
                    last.then_inc(probsT_mm[h], 1)

            def attend_values(c, halves):
                for h in halves:
                    pe.wait_ge(probsT_done[h], c + 1)
                    for i, t in enumerate(tiles_of(h)):
                        last = nc.tensor.matmul(ps_rows[h][:, i], probsT[:, t * P:(t + 1) * P], at(V2, c),
                                                start=True, stop=True)
                    last.then_inc(values_mm[h], 1)

            def transpose_xn(c, halves):
                for h in halves:
                    pe.wait_ge(xn_done[h], TB * c + TB)
                    for k in range(KD):
                        for i, t in enumerate(tiles_of(h)):
                            last = nc.tensor.transpose(ps_nT[h][:, k, i * P:(i + 1) * P], xn[:, t, k * P:(k + 1) * P],
                                                       ident[:])
                    last.then_inc(nT_mm[h], 1)

            def mlp(c, part, next_c, halves):
                before, tokens = groups_before(c, part), columns(part)
                width = tokens.stop - tokens.start
                own = both if part is None else [part]
                for m in range(KH):
                    if m >= NF:
                        pe.wait_ge(lo_done, before + m - NF + 1)
                    for i, ready in enumerate((nT_hi_done, nT_lo_done)):
                        if m == 0:
                            for h in own:
                                pe.wait_ge(ready[h], c + 1)
                        for k in range(KD):
                            last = nc.tensor.matmul(hid[m % NF][:, 0:width], W0[:, k, m * P:(m + 1) * P],
                                                    nT[i][:, k, tokens],
                                                    start=(k == 0 and i == 0), stop=(k == KD - 1 and i == 1))
                    last.then_inc(hidden_mm, 1)
                score_steps = query_score_steps(halves)
                for m in range(KH):
                    if halves and m == 2:
                        transpose_probs(next_c, halves)
                    if halves and m == 3:
                        attend_values(next_c, halves)
                    pe.wait_ge(lo_done, before + KH + m - NF + 1)
                    for i, ready in enumerate((hi_done, lo_done)):
                        for k in range(KH):
                            if m == 0:
                                pe.wait_ge(ready, before + k + 1)
                            if part == 0 and m == 0 and i == 0:
                                if k < W1_BY_ACT:
                                    pe.wait_ge(W1_by_act_done, k + 1)
                                else:
                                    pe.wait_ge(W1_done, k - W1_BY_ACT + 1)
                            last = nc.tensor.matmul(hid[m % NF][:, 0:width], W1[:, k, m * P:(m + 1) * P],
                                                    h1[i][:, k, tokens],
                                                    start=(k == 0 and i == 0), stop=(k == KH - 1 and i == 1))
                            if m == 0 and score_steps:
                                query_score(next_c, *score_steps.pop(0))
                    last.then_inc(hidden_mm, 1)
                if halves:
                    transpose_xn(next_c, halves)
                if part == 0:
                    pe.wait_ge(W2_done, 1)
                if not halves:
                    pe.wait_ge(lo_done, before + HB - NF + 1)
                for h in own:
                    for j, t in enumerate(tiles_of(h)):
                        rows = ps_rows[h][:, j] if halves else hid[t][:, 0:D]
                        for i, ready in enumerate((hi_done, lo_done)):
                            for k in range(KH):
                                if t == own[0] * TB:
                                    pe.wait_ge(ready, before + KH + k + 1)
                                last = nc.tensor.matmul(rows, h2[i][:, k, t * P:(t + 1) * P], W2[:, k],
                                                        start=(k == 0 and i == 0), stop=(k == KH - 1 and i == 1))
                        if not halves or j == TB - 1:
                            last.then_inc(rows_mm, 1)

            def product(dst, lhsT, rhs):
                for k in range(KD):
                    last = nc.tensor.matmul(dst, lhsT(k), rhs(k), start=(k == 0), stop=(k == KD - 1))
                return last

            def project_K(b):
                for m in range(KD):
                    last = product(ps_K[:, m], lambda k: wkT_sb[:, k, m * P:(m + 1) * P],
                                   lambda k: ctxT_sb[:, k, b * L:(b + 1) * L])
                last.then_inc(K_mm, 1)

            def project_V(b, tiles=range(KD)):
                for m in tiles:
                    product(ps_V[b][:, m], lambda k: wvT_sb[:, k, m * P:(m + 1) * P],
                            lambda k: ctxT_sb[:, k, b * L:(b + 1) * L]).then_inc(V_mm, 1)

            def fold_keys(b):
                pe.wait_ge(KT_done, KD * (b + 1))
                for m in range(KD):
                    last = product(ps_G[:, m], lambda k: wqc[:, k, m * P:(m + 1) * P], lambda k: KT[:, b, k])
                last.then_inc(G_mm, 1)

            def fold_bias(b):
                product(ps_qb, lambda k: bq_wide[:, k], lambda k: KT[:, b, k]).then_inc(qb_mm, 1)

            def fold_values(b):
                pe.wait_ge(VT_done, KD * (b + 1))
                product(ps_V2, lambda k: VT[:, b, k], lambda k: wfcT_sb[:, k]).then_inc(V2_mm, 1)

            def keep_busy(n, bank):
                for _ in range(n):
                    nc.tensor.matmul(bank[:, :], warm_up[:, 0:P], warm_up[:], start=True, stop=True)

            pe.wait_ge(warm_up_set, 1)
            keep_busy(WARM_UP, hid[3])

            pe.wait_ge(ctx_in, 16)
            pe.wait_ge(wk_in, 16)
            project_K(0)
            pe.wait_ge(wv_in, 16)
            project_V(0, range(1))
            pe.wait_ge(wqc_done, KD)
            fold_keys(0)
            project_V(0, range(1, KD))
            pe.wait_ge(bq_wide_done, KD)
            fold_bias(0)
            pe.wait_ge(G_done, 1)
            for step in query_score_steps([0]):
                query_score(0, *step)
            pe.wait_ge(wfc_in, 16)
            fold_values(0)
            project_K(1)
            pe.wait_ge(ident_step, 2)
            transpose_probs(0, [0])
            project_V(1)
            pe.wait_ge(V2_done, 1)
            attend_values(0, [0])
            pe.wait_ge(G_done, CB)
            fold_keys(1)
            keep_busy(4, hid[0])
            pe.wait_ge(key_bias_done, CB)
            fold_bias(1)
            pe.wait_ge(V2_done, CB)
            fold_values(1)
            keep_busy(1, hid[0])
            transpose_xn(0, [0])
            keep_busy(2, hid[0])
            pe.wait_ge(key_bias_done, NC)
            pe.wait_ge(G_done, NC)
            pe.wait_ge(V2_done, NC)
            pe.wait_ge(W0_done, 1)
            mlp(0, 0, 0, [1])
            mlp(0, 1, 1, both)
            with pe.Fori(1, NC - 1) as c:
                mlp(c, None, c + 1, both)
            mlp(NC - 1, None, None, [])



def kernel(**inputs):
    import concourse.bacc as bacc
    from concourse.bass_utils import run_bass_kernel_spmd

    a = {name: np.asarray(v) for name, v in inputs.items()}

    def tiles(m):
        return np.ascontiguousarray(m.reshape(m.shape[0] // P, P, m.shape[1]).transpose(1, 0, 2))

    x = a["x"].reshape(B * S, D)
    arrays = {
        "x": x,
        "xT": x.reshape(NC, P, HALVES, TB, KD, P).transpose(5, 0, 2, 4, 3, 1).reshape(P, NC, HALVES, KD, HALF),
        "ctxT": tiles(a["ctx_1024"].reshape(BL, D).T),
        "wkT": tiles(a["L0_xattn_Wk"][:D].T),
        "wvT": tiles(a["L0_xattn_Wk"][D:].T),
        "wq": tiles(a["L0_xattn_Wq"]),
        "wfcT": tiles(a["L0_xattn_Wfc"].T),
        "bias_cols": np.concatenate([a["L0_xattn_bk"].reshape(-1, P).T, a["L0_xattn_bq"].reshape(-1, P).T], 1),
        "bfc": a["L0_xattn_bfc"],
        "mask": a["mask_BxS2_bk0"].reshape(BL),
        "scalars": np.concatenate([a[n].reshape(1) for n in
                                   ("g_xattn", "g_ffn", "L0_ffn_s0", "L0_ffn_s1", "L0_ffn_s2")]),
        "k0": tiles(a["L0_ffn_k0"]),
        "k1": tiles(a["L0_ffn_k1"]),
        "k2": tiles(a["L0_ffn_k2"]),
    }
    arrays = {n: np.ascontiguousarray(v) for n, v in arrays.items()}
    nc = bacc.Bacc("TRN2", target_bir_lowering=False, num_devices=1)
    args = [nc.dram_tensor(n, v.shape, mybir.dt.from_np(v.dtype), kind="ExternalInput").ap()
            for n, v in arrays.items()]
    out = nc.dram_tensor("out", (B * S, D), mybir.dt.float32, kind="ExternalOutput").ap()
    flamingo_kernel(nc, *args, out)
    r = run_bass_kernel_spmd(nc, [arrays], core_ids=[0])
    return r.results[0]["out"].reshape(B, S, D)
```
